# Optimizing a Trainium2 kernel written in Bass

```python
import numpy as np
import jax
import jax.numpy as jnp

def _softmax(x, axis=-1):
    return jax.nn.softmax(x, axis=axis)

def _gelu(x):
    return jax.nn.gelu(x, approximate=True)

def _silu(x):
    return jax.nn.silu(x)

def _sigmoid(x):
    return jax.nn.sigmoid(x)

def _layernorm(x, axis=-1, eps=1e-05):
    m = jnp.mean(x, axis=axis, keepdims=True)
    v = jnp.var(x, axis=axis, keepdims=True)
    return (x - m) / jnp.sqrt(v + eps)

def _scatter_add(tgt, idx, src, axis=0):
    return tgt.at[idx].add(src)

def _segment_sum(src, seg, n):
    return jax.ops.segment_sum(src, seg, n)
kernel_name = 'mk_prb_d1_jaxref_r8_384e9b'

def setup_inputs(seed: int=0):
    np.random.seed(seed)
    _w = jnp.asarray

    def _L0_attn_setup():
        import math
        import jax, jax.numpy as jnp
        import numpy as np
        B, N, D = (4, 512, 128)
        H, M = (16, 64)
        HD = D // H
        EPS = 1e-06

        def favor_features(data, proj):
            hd = data.shape[-1]
            m = proj.shape[0]
            dn = data / math.sqrt(hd)
            norm_sq = 0.5 * jnp.sum(dn * dn, axis=-1, keepdims=True)
            comb = jnp.einsum('bhnd,md->bhnm', dn, proj) - norm_sq
            comb = comb - jnp.max(comb, axis=-1, keepdims=True)
            return jnp.exp(comb) / math.sqrt(m) + EPS
        key = jax.random.key(seed)
        ks = jax.random.split(key, 6)
        x = jax.random.normal(ks[0], (B, N, D), dtype=jnp.float32)
        qkv_w = jax.random.normal(ks[1], (3 * D, D), dtype=jnp.float32) * (1.0 / math.sqrt(D))
        qkv_b = jnp.zeros((3 * D,), dtype=jnp.float32)
        proj_w = jax.random.normal(ks[2], (D, D), dtype=jnp.float32) * (1.0 / math.sqrt(D))
        proj_b = jnp.zeros((D,), dtype=jnp.float32)
        pm = jax.random.normal(ks[3], (M, HD), dtype=jnp.float32)
        pm = pm / jnp.linalg.norm(pm, axis=-1, keepdims=True)
        return {'x': x, 'qkv_w': qkv_w, 'qkv_b': qkv_b, 'proj_w': proj_w, 'proj_b': proj_b, 'projection_matrix': pm}
    _L0_attn_in = _L0_attn_setup()

    def _L0_ffn_setup():
        import jax, jax.numpy as jnp
        import numpy as np
        E = 8
        D = 128
        H = 256
        TOP_K = 2
        key = jax.random.key(seed)
        k_x, k_g, k_w1, k_w2 = jax.random.split(key, 4)
        B, S = (4, 256)
        inp = {'input': jax.random.normal(k_x, (B, S, D), dtype=jnp.float32), 'Wg': jax.random.normal(k_g, (D, E), dtype=jnp.float32) * 0.02, 'W1': jax.random.normal(k_w1, (E, D, H), dtype=jnp.float32) * 0.02, 'b1': jnp.zeros((E, H), dtype=jnp.float32), 'W2': jax.random.normal(k_w2, (E, H, D), dtype=jnp.float32) * 0.02, 'b2': jnp.zeros((E, D), dtype=jnp.float32)}
        return inp
    _L0_ffn_in = _L0_ffn_setup()
    _d = {'L0_attn_x': _L0_attn_in['x'], 'L0_attn_qkv_w': _L0_attn_in['qkv_w'], 'L0_attn_qkv_b': _L0_attn_in['qkv_b'], 'L0_attn_proj_w': _L0_attn_in['proj_w'], 'L0_attn_proj_b': _L0_attn_in['proj_b'], 'L0_attn_projection_matrix': _L0_attn_in['projection_matrix'], 'L0_ffn_Wg': _L0_ffn_in['Wg'], 'L0_ffn_W1': _L0_ffn_in['W1'], 'L0_ffn_b1': _L0_ffn_in['b1'], 'L0_ffn_W2': _L0_ffn_in['W2'], 'L0_ffn_b2': _L0_ffn_in['b2']}
    _x0 = _d['L0_attn_x']
    _d['L0_attn_x'] = jax.random.normal(jax.random.fold_in(jax.random.key(seed), 1), (8, 1024, 128), dtype=_x0.dtype)
    del _x0
    return _d

def reference(L0_attn_x, L0_attn_qkv_w, L0_attn_qkv_b, L0_attn_proj_w, L0_attn_proj_b, L0_attn_projection_matrix, L0_ffn_Wg, L0_ffn_W1, L0_ffn_b1, L0_ffn_W2, L0_ffn_b2):

    def _L0_attn_ref(x, qkv_w, qkv_b, proj_w, proj_b, projection_matrix):
        import math
        import jax, jax.numpy as jnp
        import numpy as np
        B, N, D = (4, 512, 128)
        H, M = (16, 64)
        HD = D // H
        EPS = 1e-06

        def favor_features(data, proj):
            hd = data.shape[-1]
            m = proj.shape[0]
            dn = data / math.sqrt(hd)
            norm_sq = 0.5 * jnp.sum(dn * dn, axis=-1, keepdims=True)
            comb = jnp.einsum('bhnd,md->bhnm', dn, proj) - norm_sq
            comb = comb - jnp.max(comb, axis=-1, keepdims=True)
            return jnp.exp(comb) / math.sqrt(m) + EPS
        b, n, d = x.shape
        qkv = x @ qkv_w.T + qkv_b
        qkv = qkv.reshape(b, n, 3, H, HD)
        qkv = jnp.transpose(qkv, (2, 0, 3, 1, 4))
        q, k, v = (qkv[0], qkv[1], qkv[2])
        q_p = favor_features(q, projection_matrix)
        k_p = favor_features(k, projection_matrix)
        kv = jnp.einsum('bhnm,bhnv->bhmv', k_p, v)
        out = jnp.einsum('bhnm,bhmv->bhnv', q_p, kv)
        k_sum = jnp.sum(k_p, axis=2)
        normalizer = jnp.einsum('bhnm,bhm->bhn', q_p, k_sum)[..., None]
        out = out / (normalizer + EPS)
        out = jnp.transpose(out, (0, 2, 1, 3)).reshape(b, n, d)
        return out @ proj_w.T + proj_b

    def _L0_ffn_ref(input, Wg, W1, b1, W2, b2):
        import jax, jax.numpy as jnp
        import numpy as np
        E = 8
        D = 128
        H = 256
        TOP_K = 2
        logits = jnp.einsum('bsd,de->bse', input, Wg)
        probs = jax.nn.softmax(logits, axis=-1)
        top_vals, top_idx = jax.lax.top_k(probs, TOP_K)
        top_vals = top_vals / jnp.sum(top_vals, axis=-1, keepdims=True)
        onehot = jax.nn.one_hot(top_idx, E, dtype=input.dtype)
        mask = jnp.sum(onehot, axis=2)
        scores = jnp.sum(onehot * top_vals[..., None], axis=2)
        xm = input[None] * jnp.moveaxis(mask, -1, 0)[..., None]
        h = jnp.einsum('ebsd,edh->ebsh', xm, W1) + b1[:, None, None, :]
        h = jax.nn.relu(h)
        y = jnp.einsum('ebsh,ehd->ebsd', h, W2) + b2[:, None, None, :]
        out = jnp.sum(y * jnp.moveaxis(scores, -1, 0)[..., None], axis=0)
        return out
    x = L0_attn_x
    xn = _layernorm(x, axis=-1)
    x = x + _L0_attn_ref(xn, L0_attn_qkv_w, L0_attn_qkv_b, L0_attn_proj_w, L0_attn_proj_b, L0_attn_projection_matrix) + _L0_ffn_ref(xn, L0_ffn_Wg, L0_ffn_W1, L0_ffn_b1, L0_ffn_W2, L0_ffn_b2)
    return x

_drawn_inputs = setup_inputs


def setup_inputs(seed=0):
    import zlib

    import numpy as np

    out = dict(_drawn_inputs(seed))
    spreads = {'L0_attn_qkv_b': (0.0, 0.1),
     'L0_attn_proj_b': (0.0, 0.1),
     'L0_ffn_b1': (0.0, 0.538),
     'L0_ffn_b2': (0.0, 0.1)}
    factors = {'L0_attn_projection_matrix': 8.0}
    for name, (base, spread) in spreads.items():
        noise = np.random.default_rng([zlib.crc32(name.encode()), seed]).standard_normal(out[name].shape)
        drawn = base * np.exp(spread * noise) if base else spread * noise
        out[name] = jnp.asarray(drawn.astype(out[name].dtype))
    for name, factor in factors.items():
        out[name] = (out[name] * factor).astype(out[name].dtype)
    return out
```

```python
import concourse.bass as bass
from concourse import mybir
from contextlib import ExitStack

F32 = mybir.dt.float32
F16 = mybir.dt.float16
ALU = mybir.AluOpType
ACT = mybir.ActivationFunctionType
AX = mybir.AxisListType


def favor_moe_block(nc, x, wk2, wq2, wvg, bk2, bq2, bv, wp, bp, feat, sel, split, ident, w1, b1, w2, b2, lanes, out):
    NB, S, D = x.shape
    P = 128
    BT = 4
    BW = BT * P
    NBLK = NB * S // BW
    PER = S // BW
    H, M = 16, 64
    HD = D // H
    NH = 2
    HH = H // NH
    FW = HH * M
    NP = H // 2
    PH = NP // NH
    UN = NH * BT
    C = HD + 1
    E, HF = w1.shape[1], w1.shape[2]
    CH = E * HF // P
    EPS = 1e-6
    LIFT = 14
    LIFT_BIAS = LIFT * 0.6931471805599453
    FEAT_EPS = EPS * M ** 0.5 * 2.0 ** LIFT
    KV_SCALE = 2.0 ** -15
    DEN_EPS = EPS * M * 2.0 ** (2 * LIFT) * KV_SCALE

    xv = x.rearrange("b (k t p) d -> p (b k) t d", p=P, t=BT)
    ov = out.rearrange("b (k t p) d -> p (b k) t d", p=P, t=BT)

    with ExitStack() as ctx:
        def sb(name, shape, dt=F32):
            return ctx.enter_context(nc.sbuf_tensor(name, shape, dt))

        def sem(name):
            return ctx.enter_context(nc.semaphore(name))

        wk_sb, wq_sb = sb("wk_sb", [P, NH, P]), sb("wq_sb", [P, NH, P])
        wvg_sb = sb("wvg_sb", [P, D + E])
        bk_sb, bq_sb = sb("bk_sb", [P, NH]), sb("bq_sb", [P, NH])
        bv_sb, bp_sb = sb("bv_sb", [P, D]), sb("bp_sb", [P, D])
        wp_sb = sb("wp_sb", [P, D])
        feat_sb = sb("feat_sb", [P, FW])
        feat_hi, feat_lo = sb("feat_hi", [P, FW], F16), sb("feat_lo", [P, FW], F16)
        sel_sb = sb("sel_sb", [P, FW], F16)
        low_rows = sb("low_rows", [P, 1])
        bk_low, bq_low = sb("bk_low", [P, NH]), sb("bq_low", [P, NH])
        ident_sb = sb("ident_sb", [P, P])
        ident16 = sb("ident16", [P, P], F16)
        lift_sb = sb("lift_sb", [P, 1])
        half_pow = sb("half_pow", [P, BT])
        w1_sb = sb("w1_sb", [P, E, HF])
        b1_sb = sb("b1_sb", [P, CH])
        w2_sb = sb("w2_sb", [P, CH, D])
        b2_sb = sb("b2_sb", [P, E, D])
        lanes_sb = sb("lanes_sb", [P, E])
        acc = sb("acc", [P, NBLK, BW])
        xnT_all = sb("xnT_all", [P, NBLK, BW])
        logits = sb("logits", [P, NBLK * BT, E])
        scores = sb("scores", [P, NBLK * BT, E])
        kv_all = sb("kv_all", [P, NB, NP, 2, 2 * C], F16)
        xb = sb("xb", [P, PER, BT, D])
        xn = sb("xn", [P, BT, D])
        stat, mv = sb("stat", [P, BT, 6]), sb("mv", [P, BT, 2])
        veps, rstd = sb("veps", [P, BT]), sb("rstd", [P, BT])
        xnT = sb("xnT", [P, PER, BW])
        part_hi = sb("part_hi", [P, NH, BW], F16)
        stack = sb("stack", [P, PER, NH, BW], F16)
        v32 = sb("v32", [P, 2, 2 * P])
        v16 = sb("v16", [P, PER, BT, NP, 2, 2 * C], F16)
        NE = 4
        e_hi = sb("e_hi", [P, NE, FW], F16)
        e_32 = sb("e_32", [P, NE, FW])
        e_lo = sb("e_lo", [P, NE, FW], F16)
        mx = sb("mx", [P, NE, HH])
        mx16 = sb("mx16", [P, NE, P], F16)
        mxT = sb("mxT", [P, 2, P], F16)
        mxT_q = sb("mxT_q", [P, PER, NH, BW], F16)
        kv_low, kv32 = sb("kv_low", [P, NP, 2 * C]), sb("kv32", [P, NP, 2 * C])
        kv_now = sb("kv_now", [P, NP, 2, 2 * C], F16)
        den = sb("den", [P, 2, 2, H])
        attn = sb("attn", [P, BT, D])
        attnT = sb("attnT", [P, BW])
        res = sb("res", [P, PER, BW])
        NHT = 4
        hT = sb("hT", [P, NHT, BW])
        yb = sb("yb", [P, 2, BW])
        moe = sb("moe", [P, BW])
        bank = [ctx.enter_context(nc.psum_tensor(f"bank{n}", [P, 512], F32)) for n in range(8)]

        block = ctx.enter_context(nc.Block())
        w_in, s_const, pow_const = sem("w_in"), sem("s_const"), sem("pow_const")
        x_in = [sem(f"x_in{k}") for k in range(PER)]
        stats_done, rstd_done, xn_ready, acc_ready = sem("stats_done"), sem("rstd_done"), sem("xn_ready"), sem("acc_ready")
        xT_done, xT_kept, kT_done, khi_done, kst_ready = sem("xT_done"), sem("xT_kept"), sem("kT_done"), sem("khi_done"), sem("kst_ready")
        v_done, v_taken, vhi_done, vlo_done = sem("v_done"), sem("v_taken"), sem("vhi_done"), sem("vlo_done")
        feat_done, mx_ready, mxT_done, mxT_ready, shifted = sem("feat_done"), sem("mx_ready"), sem("mxT_done"), sem("mxT_ready"), sem("shifted")
        exp_done, dp_free, elo_ready, e_free = sem("exp_done"), sem("dp_free"), sem("elo_ready"), sem("e_free")
        kvlow_done, kv_taken, kvhi_done, kv_split = sem("kvlow_done"), sem("kv_taken"), sem("kvhi_done"), sem("kv_split")
        dve_step = sem("dve_step")
        ln_step, mx_step, qmx_step, nrm_step = sem("ln_step"), sem("mx_step"), sem("qmx_step"), sem("nrm_step")
        act_step = sem("act_step")
        routed, e2_done = sem("routed"), sem("e2_done")
        z_done, h_ready, h_free, y_taken, moe_done = sem("z_done"), sem("h_ready"), sem("h_free"), sem("y_taken"), sem("moe_done")
        qT_done, qhi_done, qst_ready = sem("qT_done"), sem("qhi_done"), sem("qst_ready")
        qf_done, qmx_ready, qmxT_done, qmxT_ready = sem("qf_done"), sem("qmx_ready"), sem("qmxT_done"), sem("qmxT_ready")
        qs_done, qexp_done, qlo_ready, qe_free, qs_free = sem("qs_done"), sem("qexp_done"), sem("qlo_ready"), sem("qe_free"), sem("qs_free")
        kv_now_ready, attn_ready, aT_done, aT_ready, proj_done, res_ready = (
            sem("kv_now_ready"), sem("attn_ready"), sem("aT_done"), sem("aT_ready"), sem("proj_done"), sem("res_ready"))
        out_done = [sem(f"out_done{k}") for k in range(PER)]

        dp = bank[0:4]
        xk, vb, mt, kvb = bank[4], bank[5], bank[6], bank[7]
        mt16 = mt[:, 0:64].bitcast(F16)
        kv_ps = kvb[:, 0:NP * 4 * C].rearrange("p (n s c) -> p n s c", n=NP, s=2)
        tm, fm, ob = bank[0:2], bank[2:4], bank[4:6]
        qb = bank[7]

        WAITS_W = 16 * 17

        def load_weights(eng):
            for dst, src in ((wk_sb[:], wk2), (wvg_sb[:], wvg), (bk_sb[:], bk2), (low_rows[:], split),
                             (feat_sb[:], feat), (sel_sb[:], sel), (ident_sb[:], ident), (bv_sb[:], bv),
                             (bp_sb[:], bp), (wq_sb[:], wq2), (bq_sb[:], bq2), (wp_sb[:], wp),
                             (w1_sb[:], w1), (b1_sb[:], b1), (w2_sb[:], w2), (b2_sb[:], b2), (lanes_sb[:], lanes)):
                eng.dma_start(dst, src).then_inc(w_in, 16)

        def over_batches(eng, first, body):
            first()
            with eng.Fori(0, NB - 1) as i:
                for k in range(PER):
                    body(i, k, i if k + 1 < PER else i + 1, (k + 1) % PER)
            for k in range(PER):
                if k + 1 < PER:
                    body(NB - 1, k, NB - 1, k + 1)
                else:
                    body(NB - 1, k, None, None)

        ONE = 1
        from_one = [kv_taken, mxT_ready, kv_split, attn_ready, aT_done, res_ready, y_taken] + out_done

        @block.sync
        def _(sp):
            for s in from_one:
                nc.sync.sem_inc(s, ONE)
            for k in range(PER):
                sp.dma_start(xb[:, k], xv[:, k]).then_inc(x_in[k], 16)
            load_weights(sp)
            with sp.Fori(1, NB) as i:
                for k in range(PER):
                    sp.wait_ge(xn_ready, PER * i + k - PER + 1)
                    sp.wait_ge(acc_ready, PER * i + k - PER + 1)
                    sp.dma_start(xb[:, k], xv[:, bass.ds(PER * i + k, 1)].rearrange("p o t d -> p (o t) d")).then_inc(x_in[k], 16)
            with sp.Fori(0, NB) as i:
                for k in range(PER):
                    sp.wait_ge(res_ready, ONE + PER * i + k + 1)
                    sp.dma_start(ov[:, bass.ds(PER * i + k, 1)].rearrange("p o t d -> p (o t) d"),
                                 res[:, k].rearrange("p (t d) -> p t d", t=BT)).then_inc(out_done[k], 16)
            for k in range(PER):
                sp.wait_ge(out_done[k], ONE + 16 * NB)

        @block.gpsimd
        def _(pool):
            nc.gpsimd.memset(half_pow[:], -0.5).then_inc(pow_const, 1)
            pool.wait_ge(pow_const, 1)
            pool.wait_ge(s_const, 2)
            pool.wait_ge(w_in, WAITS_W)

            def prep(i, k):
                b = PER * i + k
                pool.wait_ge(stats_done, b + 1)
                nc.gpsimd.tensor_tensor(out=rstd[:], in0=veps[:], in1=half_pow[:], op=ALU.pow).then_inc(rstd_done, 1)
                pool.wait_ge(x_in[k], 16 * i + 16)
                nc.gpsimd.tensor_tensor(out=acc[:, bass.ds(b, 1)].rearrange("p o (t d) -> p (o t) d", d=D), in0=xb[:, k],
                                        in1=bp_sb[:].unsqueeze(1).to_broadcast([P, BT, D]), op=ALU.add).then_inc(acc_ready, 1)
                for j in range(2):
                    pool.wait_ge(vhi_done, 2 * b + j + 1)
                    d = v16[:, k, 2 * j:2 * j + 2].rearrange("p t n s (h c) -> p (t n) s h c", h=2)
                    nc.gpsimd.tensor_tensor(out=d[:, :, 1, :, 0:HD], in0=v32[:, j].rearrange("p (n h c) -> p n h c", h=2, c=HD),
                                            in1=d[:, :, 0, :, 0:HD], op=ALU.subtract).then_inc(vlo_done, 1)

            def body(i, k, pi, pk):
                if pi is not None:
                    prep(pi, pk)

            over_batches(pool, lambda: prep(0, 0), body)

        @block.scalar
        def _(act):
            nc.scalar.sem_inc(dp_free, 4)
            act.wait_ge(w_in, WAITS_W)
            act.wait_ge(s_const, 2)

            def prep_xT(i, k):
                b = PER * i + k
                act.wait_ge(xT_done, b + 1)
                nc.scalar.activation(xnT[:, k], xk[:, :], ACT.Copy)
                nc.scalar.activation(xnT_all[:, bass.ds(b, 1)].rearrange("p o n -> p (o n)"), xk[:, :], ACT.Copy).then_inc(xT_kept, 1)

            def prep_hi(i, k, a):
                act.wait_ge(kT_done, NH * (PER * i + k) + a + 1)
                nc.scalar.activation(part_hi[:, a], xk[:, :], ACT.Identity, scale=low_rows[:, 0:1],
                                     bias=bk_low[:, a:a + 1]).then_inc(khi_done, 1)

            def prep_v(i, k, j):
                act.wait_ge(v_taken, 2 * (PER * i + k) + j + 1)
                d = v16[:, k, 2 * j:2 * j + 2].rearrange("p t n s (h c) -> p (t n) s h c", h=2)
                nc.scalar.activation(d[:, :, 0, :, 0:HD], v32[:, j].rearrange("p (n h c) -> p n h c", h=2, c=HD),
                                     ACT.Copy).then_inc(vhi_done, 1)

            def body(i, k, pi, pk):
                b = PER * i + k
                for s in range(UN + 3):
                    if 1 <= s <= UN:
                        u = s - 1
                        act.wait_ge(mxT_done, UN * b + u + 1)
                        nc.scalar.activation(mxT[:, u % 2], mt16, ACT.Copy).then_inc(mxT_ready, 1)
                    if 2 <= s <= UN + 1:
                        u = s - 2
                        act.wait_ge(shifted, UN * b + u + 1)
                        act.wait_ge(e_free, UN * b + u + 1)
                        nc.scalar.activation(e_hi[:, u % NE], dp[u % 4][:, :], ACT.Exp, bias=lift_sb[:, 0:1])
                        nc.scalar.activation(e_32[:, u % NE], dp[u % 4][:, :], ACT.Exp, bias=lift_sb[:, 0:1])\
                            .then_inc(dp_free, 1)
                    if pi is not None:
                        if s == 5:
                            prep_xT(pi, pk)
                        if s == 7:
                            prep_hi(pi, pk, 0)
                        if s == 9:
                            prep_hi(pi, pk, 1)
                        if s == 10:
                            prep_v(pi, pk, 0)
                            prep_v(pi, pk, 1)
                if k == PER - 1:
                    act.wait_ge(e_free, NE + UN * PER * (i + 1))
                    nc.scalar.activation(kv_low[:], kv_ps[:, :, 1, :], ACT.Copy, scale=KV_SCALE).then_inc(kvlow_done, 1)
                    act.wait_ge(kv_taken, ONE + i + 1)
                    kd = kv_all[:, bass.ds(i, 1)].rearrange("p o n s c -> p (o n) s c")
                    for g in range(2):
                        r, c = slice(64 * g, 64 * g + 64), slice(C * g, C * g + C)
                        nc.scalar.activation(kd[r, :, 0, c], kv32[r, :, c], ACT.Copy).then_inc(kvhi_done, 1)

            def first():
                prep_xT(0, 0)
                prep_hi(0, 0, 0)
                prep_hi(0, 0, 1)
                prep_v(0, 0, 0)
                prep_v(0, 0, 1)

            over_batches(act, first, body)

            act.wait_ge(routed, 1)
            nt = NBLK * BT
            nc.scalar.activation(res[:, 0, 3 * nt:4 * nt], res[:, 0, 4 * nt:5 * nt], ACT.Exp).then_inc(e2_done, 1)

            with act.Fori(0, NBLK) as b:
                for c in range(CH):
                    act.wait_ge(z_done, CH * b + c + 1)
                    act.wait_ge(h_free, CH * b + c + 1)
                    nc.scalar.activation(hT[:, c % NHT], bank[c % 4][:, :], ACT.Relu, bias=b1_sb[:, c:c + 1]).then_inc(h_ready, 1)

            nc.scalar.sem_inc(qs_free, 2)
            def qprep(i, k, a):
                act.wait_ge(qT_done, NH * (PER * i + k) + a + 1)
                nc.scalar.activation(part_hi[:, a], qb[:, :], ACT.Identity, scale=low_rows[:, 0:1],
                                     bias=bq_low[:, a:a + 1]).then_inc(qhi_done, 1)

            def qmxT(i, k, u):
                act.wait_ge(qmxT_done, UN * (PER * i + k) + u + 1)
                a, t = divmod(u, BT)
                nc.scalar.activation(mxT_q[:, k, a, t * P:(t + 1) * P], mt16, ACT.Copy).then_inc(qmxT_ready, 1)

            def qbody(i, k, pi, pk):
                b = PER * i + k
                for s in range(UN + 4):
                    if s < NP:
                        act.wait_ge(qs_done, NP * b + s + 1)
                        act.wait_ge(qe_free, NP * b + s + 1)
                        nc.scalar.activation(e_hi[:, s % NE], fm[s % 2][:, :], ACT.Exp, bias=lift_sb[:, 0:1])
                        nc.scalar.activation(e_32[:, s % NE], fm[s % 2][:, :], ACT.Exp, bias=lift_sb[:, 0:1])\
                            .then_inc(qs_free, 1)
                    if pi is not None:
                        if s < NH:
                            qprep(pi, pk, s)
                        if s >= 3 and s - 3 < UN:
                            qmxT(pi, pk, s - 3)
                if pi is not None:
                    qmxT(pi, pk, UN - 1) if UN + 4 - 3 < UN else None
                act.wait_ge(aT_done, ONE + b + 1)
                nc.scalar.activation(attnT[:], qb[:, :], ACT.Copy).then_inc(aT_ready, 1)

            def qfirst():
                for a in range(NH):
                    qprep(0, 0, a)
                for u in range(UN):
                    qmxT(0, 0, u)

            over_batches(act, qfirst, qbody)

        @block.vector
        def _(dve):
            steps = [0]

            nc.vector.memset(lift_sb[:], LIFT_BIAS)
            nc.vector.memset(mx16[:], 0.0)
            nc.vector.memset(kv_all[:], 0.0)
            nc.vector.memset(v16[:, :, :, :, 1], 0.0)
            nc.vector.memset(v16[:, :, :, :, 0], 1.0).then_inc(s_const, 1)
            dve.wait_ge(w_in, WAITS_W)
            nc.vector.tensor_copy(ident16[:], ident_sb[:])
            nc.vector.tensor_tensor(out=bk_low[:], in0=bk_sb[:], in1=low_rows[:].to_broadcast([P, NH]), op=ALU.mult)
            nc.vector.tensor_tensor(out=bq_low[:], in0=bq_sb[:], in1=low_rows[:].to_broadcast([P, NH]), op=ALU.mult)
            nc.vector.tensor_scalar(out=e_32[:, 0], in0=feat_sb[:], scalar1=float(HD) ** -0.5, scalar2=None, op0=ALU.mult).then_inc(dve_step, 1)
            dve.wait_ge(dve_step, 1)
            nc.vector.tensor_copy(feat_hi[:], e_32[:, 0]).then_inc(dve_step, 1)
            dve.wait_ge(dve_step, 2)
            nc.vector.tensor_tensor(out=feat_lo[:], in0=e_32[:, 0], in1=feat_hi[:], op=ALU.subtract).then_inc(s_const, 1)

            SETUP = 2
            PREP = 2
            MAIN = 2 * UN

            def stats(i, k):
                b = PER * i + k
                dve.wait_ge(x_in[k], 16 * i + 16)
                dve.wait_ge(rstd_done, b)
                for t in range(BT):
                    last = nc.vector.bn_stats(out=stat[:, t], in_=xb[:, k, t])
                last.then_inc(ln_step, 1)

            def stats_seen(i, k):
                dve.wait_ge(ln_step, 2 * (PER * i + k) + 1)

            def variance(i, k):
                b = PER * i + k
                for t in range(BT):
                    last = nc.vector.bn_aggr(out=mv[:, t], in_=stat[:, t])
                last.then_inc(ln_step, 1)
                dve.wait_ge(ln_step, 2 * b + 2)
                nc.vector.tensor_scalar(out=veps[:], in0=mv[:, :, 1], scalar1=1e-5, scalar2=None, op0=ALU.add).then_inc(stats_done, 1)

            def normalise(i, k):
                b = PER * i + k
                dve.wait_ge(rstd_done, b + 1)
                dve.wait_ge(xT_done, b)
                for t in range(BT):
                    last = nc.vector.tensor_scalar(out=xn[:, t], in0=xb[:, k, t], scalar1=mv[:, t, 0:1],
                                                   scalar2=rstd[:, t:t + 1], op0=ALU.subtract, op1=ALU.mult)
                last.then_inc(xn_ready, 1)

            def kstack(i, k, a):
                b = PER * i + k
                dve.wait_ge(khi_done, NH * b + a + 1)
                nc.vector.scalar_tensor_tensor(out=stack[:, k, a], in0=xk[:, :], scalar=bk_sb[:, a:a + 1], in1=part_hi[:, a],
                                               op0=ALU.add, op1=ALU.subtract).then_inc(kst_ready, 1)

            def values(i, k, j):
                b = PER * i + k
                dve.wait_ge(v_done, 2 * b + j + 1)
                if not (type(b) is int and b == 0):
                    dve.wait_ge(vlo_done, 2 * b + j - 1)
                vp = vb[:, 0:2 * (D + E)].rearrange("p (t c) -> p t c", t=2)
                nc.vector.tensor_tensor(out=v32[:, j].rearrange("p (t c) -> p t c", t=2), in0=vp[:, :, 0:D],
                                        in1=bv_sb[:].unsqueeze(1).to_broadcast([P, 2, D]), op=ALU.add)
                nc.vector.tensor_copy(logits[:, bass.ds(BT * b + 2 * j, 2)], vp[:, :, D:D + E]).then_inc(v_taken, 1)

            def maxima(dps, done, ready, base, u, own, own_base):
                dve.wait_ge(done, base + u + 1)
                nc.vector.tensor_reduce(out=mx[:, u % NE], in_=dps[:, :].rearrange("p (h m) -> p h m", h=HH), axis=AX.X,
                                        op=ALU.max, negate=True).then_inc(own, 1)

            def split_max(base, u, ready, own):
                dve.wait_ge(own, 2 * (base + u) + 1)
                nc.vector.tensor_copy(mx16[:, u % NE, 0:HH], mx[:, u % NE]).then_inc(own, 1)
                dve.wait_ge(own, 2 * (base + u) + 2)
                nc.vector.tensor_tensor(out=mx16[:, u % NE, HH:2 * HH], in0=mx[:, u % NE], in1=mx16[:, u % NE, 0:HH],
                                        op=ALU.subtract).then_inc(ready, 1)

            def low_part(n, done, count, ready):
                dve.wait_ge(done, count)
                nc.vector.scalar_tensor_tensor(out=e_lo[:, n % NE], in0=e_32[:, n % NE], scalar=FEAT_EPS, in1=e_hi[:, n % NE],
                                               op0=ALU.add, op1=ALU.subtract).then_inc(ready, 1)

            def body(i, k, pi, pk):
                b = PER * i + k
                for s in range(UN + 3):
                    if s == 1 and pi is not None:
                        stats_seen(pi, pk)
                    if s < UN:
                        maxima(dp[s % 4], feat_done, mx_ready, UN * b, s, mx_step, None)
                    if 3 <= s:
                        low_part(s - 3, dp_free, 4 + UN * b + s - 3 + 1, elo_ready)
                    if s < UN:
                        split_max(UN * b, s, mx_ready, mx_step)
                    if pi is not None:
                        if s == 0:
                            stats(pi, pk)
                        if s == 1:
                            variance(pi, pk)
                        if s == 2:
                            normalise(pi, pk)
                        if s == 8:
                            kstack(pi, pk, 0)
                        if s == 10:
                            kstack(pi, pk, 1)
                            values(pi, pk, 0)
                            values(pi, pk, 1)
                if k == PER - 1:
                    dve.wait_ge(kv_split, ONE + 2 * i)
                    dve.wait_ge(kvlow_done, i + 1)
                    nc.vector.scalar_tensor_tensor(out=kv32[:], in0=kv_ps[:, :, 0, :], scalar=KV_SCALE, in1=kv_low[:],
                                                   op0=ALU.mult, op1=ALU.add).then_inc(kv_taken, 1)
                    kd = kv_all[:, bass.ds(i, 1)].rearrange("p o n s c -> p (o n) s c")
                    dve.wait_ge(kvhi_done, 2 * i + 2)
                    for g in range(2):
                        r, c = slice(64 * g, 64 * g + 64), slice(C * g, C * g + C)
                        nc.vector.tensor_tensor(out=kd[r, :, 1, c], in0=kv32[r, :, c], in1=kd[r, :, 0, c],
                                                op=ALU.subtract).then_inc(kv_split, 1)

            def first():
                stats(0, 0)
                stats_seen(0, 0)
                variance(0, 0)
                normalise(0, 0)
                kstack(0, 0, 0)
                kstack(0, 0, 1)
                values(0, 0, 0)
                values(0, 0, 1)

            over_batches(dve, first, body)

            NT = NBLK * BT
            n = [SETUP]

            def link(ins):
                n[0] += 1
                ins.then_inc(dve_step, 1)
                dve.wait_ge(dve_step, n[0])

            lanes_bc = lanes_sb[:].unsqueeze(1).to_broadcast([P, NT, E])
            one = [e_32[:, 0].rearrange("p (t e) -> p t e", e=E), e_32[:, 1].rearrange("p (t e) -> p t e", e=E)]
            tmp = e_32[:, 2].rearrange("p (t e) -> p t e", e=E)
            lg2 = e_32[:, 3].rearrange("p (t e) -> p t e", e=E)
            top = [res[:, 0, 0:NT], res[:, 0, NT:2 * NT]]
            key = res[:, 0, 2 * NT:3 * NT]
            dve.wait_ge(elo_ready, NBLK * UN)
            src = logits[:]
            for r in range(2):
                bc = lambda v: v.unsqueeze(2).to_broadcast([P, NT, E])
                link(nc.vector.tensor_reduce(out=top[r], in_=src, axis=AX.X, op=ALU.max))
                link(nc.vector.tensor_tensor(out=tmp, in0=src, in1=bc(top[r]), op=ALU.is_equal))
                link(nc.vector.tensor_tensor(out=tmp, in0=tmp, in1=lanes_bc, op=ALU.mult))
                link(nc.vector.tensor_reduce(out=key, in_=tmp, axis=AX.X, op=ALU.max))
                link(nc.vector.tensor_tensor(out=one[r], in0=lanes_bc, in1=bc(key), op=ALU.is_equal))
                if r == 0:
                    link(nc.vector.scalar_tensor_tensor(out=lg2, in0=one[0], scalar=-3e38, in1=src, op0=ALU.mult, op1=ALU.add))
                    src = lg2
            e2 = res[:, 0, 3 * NT:4 * NT]
            gap, tot = res[:, 0, 4 * NT:5 * NT], res[:, 0, 5 * NT:6 * NT]
            nc.vector.tensor_tensor(out=gap, in0=top[1], in1=top[0], op=ALU.subtract).then_inc(routed, 1)
            dve.wait_ge(e2_done, 1)
            link(nc.vector.tensor_scalar(out=tot, in0=e2, scalar1=1.0, scalar2=None, op0=ALU.add))
            link(nc.vector.reciprocal(tot, tot))
            link(nc.vector.tensor_tensor(out=e2, in0=e2, in1=tot, op=ALU.mult))
            link(nc.vector.tensor_tensor(out=one[1], in0=one[1], in1=bc(e2), op=ALU.mult))
            link(nc.vector.tensor_tensor(out=one[0], in0=one[0], in1=bc(tot), op=ALU.mult))
            link(nc.vector.tensor_tensor(out=scores[:], in0=one[0], in1=one[1], op=ALU.add))

            dve.wait_ge(acc_ready, NBLK)
            with dve.Fori(0, NBLK) as b:
                for e in range(E):
                    dve.wait_ge(h_free, NHT + 2 * (E * b + e + 1))
                    nc.vector.tensor_tensor(out=yb[:, e % 2].rearrange("p (t d) -> p t d", t=BT), in0=bank[4 + e % 2][:, :].rearrange("p (t d) -> p t d", t=BT),
                                            in1=b2_sb[:, e].unsqueeze(1).to_broadcast([P, BT, D]), op=ALU.add).then_inc(y_taken, 1)
                    dve.wait_ge(y_taken, ONE + E * b + e + 1)
                    for t in range(BT):
                        c = slice(t * P, (t + 1) * P)
                        sc = scores[:, bass.ds(BT * b + t, 1), e]
                        prev = acc[:, bass.ds(b, 1), c].rearrange("p o n -> p (o n)") if e == 0 else moe[:, c]
                        dst = acc[:, bass.ds(b, 1), c].rearrange("p o n -> p (o n)") if e == E - 1 else moe[:, c]
                        if e:
                            dve.wait_ge(moe_done, BT * (E * b + e - 1) + t + 1)
                        nc.vector.scalar_tensor_tensor(out=dst, in0=yb[:, e % 2, c], scalar=sc, in1=prev,
                                                       op0=ALU.mult, op1=ALU.add).then_inc(moe_done, 1)

            def qstack(i, k, a):
                b = PER * i + k
                dve.wait_ge(qhi_done, NH * b + a + 1)
                nc.vector.scalar_tensor_tensor(out=stack[:, k, a], in0=qb[:, :], scalar=bq_sb[:, a:a + 1], in1=part_hi[:, a],
                                               op0=ALU.add, op1=ALU.subtract).then_inc(qst_ready, 1)

            def qbody(i, k, pi, pk):
                b = PER * i + k
                if k == 0:
                    dve.wait_ge(kv_split, ONE + 2 * NB)
                    dve.wait_ge(qe_free, NE + NP * b)
                    nc.vector.tensor_copy(kv_now[:].rearrange("p n s c -> p (n s c)"),
                                          kv_all[:, bass.ds(i, 1)].rearrange("p o n s c -> p (o n s c)")).then_inc(kv_now_ready, 1)
                for s in range(UN + 3):
                    if pi is not None and s < NH:
                        qstack(pi, pk, s)
                    if 2 <= s < UN + 2 and pi is not None:
                        maxima(tm[s % 2], qf_done, qmx_ready, UN * (PER * pi + pk), s - 2, qmx_step, None)
                    if 1 <= s <= NP:
                        low_part(s - 1, qs_free, 2 + NP * b + s, qlo_ready)
                    if 2 <= s < UN + 2 and pi is not None:
                        split_max(UN * (PER * pi + pk), s - 2, qmx_ready, qmx_step)
                dve.wait_ge(qe_free, NE + NP * (b + 1))
                dve.wait_ge(aT_done, ONE + b)
                o4 = [o[:, 0:2 * H * C].rearrange("p (t h c) -> p t h c", t=2, c=C) for o in ob]
                for g in range(2):
                    last = nc.vector.tensor_scalar(out=den[:, g], in0=o4[g][:, :, :, HD], scalar1=DEN_EPS, scalar2=None, op0=ALU.add)
                last.then_inc(nrm_step, 1)
                dve.wait_ge(nrm_step, 2 * b + 1)
                nc.vector.reciprocal(den[:], den[:]).then_inc(nrm_step, 1)
                dve.wait_ge(nrm_step, 2 * b + 2)
                for g in range(2):
                    last = nc.vector.tensor_tensor(out=attn[:, 2 * g:2 * g + 2].rearrange("p t (h c) -> p t h c", c=HD),
                                                   in0=o4[g][:, :, :, 0:HD], in1=den[:, g].unsqueeze(3).to_broadcast([P, 2, H, HD]), op=ALU.mult)
                last.then_inc(attn_ready, 1)
                dve.wait_ge(proj_done, b + 1)
                if not (type(i) is int and i == 0):
                    dve.wait_ge(out_done[k], ONE + 16 * i)
                nc.vector.tensor_tensor(out=res[:, k], in0=qb[:, :], in1=acc[:, bass.ds(b, 1)].rearrange("p o n -> p (o n)"),
                                        op=ALU.add).then_inc(res_ready, 1)

            def qfirst():
                for a in range(NH):
                    qstack(0, 0, a)
                for u in range(UN):
                    maxima(tm[u % 2], qf_done, qmx_ready, 0, u, qmx_step, None)
                    split_max(0, u, qmx_ready, qmx_step)

            over_batches(dve, qfirst, qbody)

        @block.tensor
        def _(pe):
            nc.tensor.sem_inc(e_free, NE)
            pe.wait_ge(s_const, 2)
            pe.wait_ge(w_in, WAITS_W)
            mm = nc.tensor.matmul

            def prep_xT(i, k):
                b = PER * i + k
                pe.wait_ge(xn_ready, b + 1)
                pe.wait_ge(kst_ready, NH * b)
                for t in range(BT):
                    last = nc.tensor.transpose(xk[:, t * P:(t + 1) * P], xn[:, t], ident_sb[:])
                last.then_inc(xT_done, 1)

            def prep_kT(i, k, a):
                b = PER * i + k
                if a == 0:
                    pe.wait_ge(xT_kept, b + 1)
                else:
                    pe.wait_ge(kst_ready, NH * b + a)
                mm(xk[:, :], wk_sb[:, a], xnT[:, k], start=True, stop=True).then_inc(kT_done, 1)

            def prep_v(i, k, j):
                b = PER * i + k
                pe.wait_ge(v_taken, 2 * b + j)
                for t in range(2):
                    w = D + E
                    last = mm(vb[:, t * w:(t + 1) * w], xnT[:, k, (2 * j + t) * P:(2 * j + t + 1) * P], wvg_sb[:],
                              start=(t == 0), stop=(t == 1), skip_group_check=True)
                last.then_inc(v_done, 1)

            def body(i, k, pi, pk):
                b = PER * i + k
                for s in range(UN + 3):
                    if s < UN:
                        a, t = divmod(s, BT)
                        if t == 0:
                            pe.wait_ge(kst_ready, NH * b + a + 1)
                        pe.wait_ge(dp_free, UN * b + s + 1)
                        w = stack[:, k, a, t * P:(t + 1) * P]
                        mm(dp[s % 4][:, :], w, feat_hi[:], start=True, stop=False, skip_group_check=True)
                        mm(dp[s % 4][:, :], w, feat_lo[:], start=False, stop=False, skip_group_check=True).then_inc(feat_done, 1)
                    if 1 <= s <= UN:
                        u = s - 1
                        pe.wait_ge(mx_ready, UN * b + u + 1)
                        pe.wait_ge(mxT_ready, ONE + UN * b + u)
                        nc.tensor.transpose(mt16, mx16[:, u % NE], ident16[:]).then_inc(mxT_done, 1)
                    if 2 <= s <= UN + 1:
                        u = s - 2
                        pe.wait_ge(mxT_ready, ONE + UN * b + u + 1)
                        mm(dp[u % 4][:, :], mxT[:, u % 2], sel_sb[:], start=False, stop=True, skip_group_check=True).then_inc(shifted, 1)
                    if 3 <= s:
                        u = s - 3
                        a, t = divmod(u, BT)
                        pe.wait_ge(elo_ready, UN * b + u + 1)
                        pe.wait_ge(vlo_done, 2 * b + t // 2 + 1)
                        if k == 0 and u == 0:
                            pe.wait_ge(kv_taken, ONE + i)
                        for n in range(PH):
                            pr = a * PH + n
                            mm(kv_ps[:, pr].rearrange("p s c -> p (s c)"), e_hi[:, u % NE, n * P:(n + 1) * P],
                               v16[:, k, t, pr].rearrange("p s c -> p (s c)"), start=(k == 0 and u == 0 and n == 0),
                               stop=False, skip_group_check=True)
                            last = mm(kv_ps[:, pr, 0], e_lo[:, u % NE, n * P:(n + 1) * P], v16[:, k, t, pr, 0],
                                      start=False, stop=(k == PER - 1 and u == UN - 1 and n == PH - 1), skip_group_check=True)
                        last.then_inc(e_free, 1)
                    if pi is not None:
                        if s == 5:
                            prep_xT(pi, pk)
                        if s == 7:
                            prep_kT(pi, pk, 0)
                        if s == 8:
                            prep_kT(pi, pk, 1)
                        if s == 9:
                            prep_v(pi, pk, 0)
                        if s == 10:
                            prep_v(pi, pk, 1)

            def first():
                prep_xT(0, 0)
                prep_kT(0, 0, 0)
                prep_kT(0, 0, 1)
                prep_v(0, 0, 0)
                prep_v(0, 0, 1)

            over_batches(pe, first, body)

            nc.tensor.sem_inc(h_free, NHT)
            pe.wait_ge(kv_split, ONE + 2 * NB)
            with pe.Fori(0, NBLK) as b:
                for c in range(CH + 2):
                    if c < CH:
                        pe.wait_ge(h_free, CH * b + c + 1)
                        mm(bank[c % 4][:, :], w1_sb[:, c // 2, (c % 2) * P:(c % 2 + 1) * P],
                           xnT_all[:, bass.ds(b, 1)].rearrange("p o n -> p (o n)"), start=True, stop=True).then_inc(z_done, 1)
                    if c >= 2 and c % 2 == 0 or c == CH + 1:
                        pass
                    if c >= 3 and c % 2 == 1:
                        e = (c - 3) // 2
                        pe.wait_ge(h_ready, CH * b + 2 * e + 2)
                        g = E * b + e
                        if e < 2:
                            pe.wait_ge(y_taken, ONE + E * b)
                        else:
                            pe.wait_ge(y_taken, ONE + g - 1)
                        for t in range(BT):
                            for r in range(2):
                                last = mm(bank[4 + e % 2][:, t * P:(t + 1) * P], hT[:, (2 * e + r) % NHT, t * P:(t + 1) * P],
                                          w2_sb[:, 2 * e + r], start=(t == 0 and r == 0), stop=(t == BT - 1 and r == 1), skip_group_check=True)
                        last.then_inc(h_free, 2)

            nc.tensor.sem_inc(qe_free, NE)
            pe.wait_ge(moe_done, BT * E * NBLK)

            def qT(i, k, a):
                b = PER * i + k
                pe.wait_ge(qst_ready, NH * b + a)
                if k or not (type(i) is int and i == 0):
                    pe.wait_ge(res_ready, ONE + b - 1)
                mm(qb[:, :], wq_sb[:, a], xnT_all[:, bass.ds(b, 1)].rearrange("p o n -> p (o n)"), start=True, stop=True).then_inc(qT_done, 1)

            def qfeat(i, k, u):
                b = PER * i + k
                a, t = divmod(u, BT)
                if t == 0:
                    pe.wait_ge(qst_ready, NH * b + a + 1)
                if u >= 2:
                    pe.wait_ge(qmx_ready, UN * b + u - 1)
                w = stack[:, k, a, t * P:(t + 1) * P]
                mm(tm[u % 2][:, :], w, feat_hi[:], start=True, stop=False)
                mm(tm[u % 2][:, :], w, feat_lo[:], start=False, stop=True).then_inc(qf_done, 1)

            def qtr(i, k, u):
                b = PER * i + k
                pe.wait_ge(qmx_ready, UN * b + u + 1)
                pe.wait_ge(qmxT_ready, UN * b + u)
                nc.tensor.transpose(mt16, mx16[:, u % NE], ident16[:]).then_inc(qmxT_done, 1)

            def qbody(i, k, pi, pk):
                b = PER * i + k
                for s in range(UN + 3):
                    if s < NP:
                        a, n = divmod(s, PH)
                        if n == 0:
                            pe.wait_ge(qmxT_ready, UN * b + (a + 1) * BT)
                        pe.wait_ge(qs_free, NP * b + s + 1)
                        f = slice(n * P, (n + 1) * P)
                        mm(fm[s % 2][:, :], feat_hi[:, f], stack[:, k, a], start=True, stop=False)
                        mm(fm[s % 2][:, :], feat_lo[:, f], stack[:, k, a], start=False, stop=False)
                        mm(fm[s % 2][:, :], sel_sb[:, f], mxT_q[:, k, a], start=False, stop=True).then_inc(qs_done, 1)
                    if pi is not None:
                        if s < NH:
                            qT(pi, pk, s)
                        if 2 <= s < UN + 2:
                            qfeat(pi, pk, s - 2)
                        if 3 <= s:
                            qtr(pi, pk, s - 3)
                    if 2 <= s < NP + 2:
                        pr = s - 2
                        pe.wait_ge(qlo_ready, NP * b + pr + 1)
                        if pr == 0:
                            pe.wait_ge(attn_ready, ONE + b)
                            if k == 0:
                                pe.wait_ge(kv_now_ready, i + 1)
                        for t in range(BT):
                            o = ob[t // 2][:, (t % 2) * H * C + pr * 2 * C:(t % 2) * H * C + (pr + 1) * 2 * C]
                            c = slice(t * P, (t + 1) * P)
                            mm(o, e_hi[:, pr % NE, c], kv_now[:, pr, 0], start=(pr == 0 and t % 2 == 0), stop=False, skip_group_check=True)
                            mm(o, e_hi[:, pr % NE, c], kv_now[:, pr, 1], start=False, stop=False, skip_group_check=True)
                            last = mm(o, e_lo[:, pr % NE, c], kv_now[:, pr, 0], start=False, stop=(pr == NP - 1 and t % 2 == 1), skip_group_check=True)
                        last.then_inc(qe_free, 1)
                if pi is not None:
                    pe.wait_ge(qst_ready, NH * (PER * pi + pk) + NH)
                pe.wait_ge(attn_ready, ONE + b + 1)
                for t in range(BT):
                    last = nc.tensor.transpose(qb[:, t * P:(t + 1) * P], attn[:, t], ident_sb[:])
                last.then_inc(aT_done, 1)
                pe.wait_ge(aT_ready, b + 1)
                for t in range(BT):
                    last = mm(qb[:, t * P:(t + 1) * P], attnT[:, t * P:(t + 1) * P], wp_sb[:], start=(t == 0), stop=(t == BT - 1), skip_group_check=True)
                last.then_inc(proj_done, 1)

            def qfirst():
                for a in range(NH):
                    qT(0, 0, a)
                for u in range(UN):
                    qfeat(0, 0, u)
                    qtr(0, 0, u)

            over_batches(pe, qfirst, qbody)


_SHAPES = dict(D=128, H=16, M=64, E=8, HF=256)


def kernel(L0_attn_x, L0_attn_qkv_w, L0_attn_qkv_b, L0_attn_proj_w, L0_attn_proj_b, L0_attn_projection_matrix,
           L0_ffn_Wg, L0_ffn_W1, L0_ffn_b1, L0_ffn_W2, L0_ffn_b2):
    import numpy as np
    import concourse.bacc as bacc
    from concourse.bass_utils import run_bass_kernel_spmd
    D, H, M, E, HF = (_SHAPES[k] for k in ("D", "H", "M", "E", "HF"))
    HD, HH = D // H, H // 2
    a = [np.asarray(v) for v in (L0_attn_x, L0_attn_qkv_w, L0_attn_qkv_b, L0_attn_proj_w, L0_attn_proj_b,
                                 L0_attn_projection_matrix, L0_ffn_Wg, L0_ffn_W1, L0_ffn_b1, L0_ffn_W2, L0_ffn_b2)]
    x, qkv_w, qkv_b, proj_w, proj_b, pm, wg, w1, b1, w2, b2 = a

    def twice(w):
        h = w.reshape(2, D // 2, -1)
        return np.concatenate([h, h], axis=1)

    feat = np.zeros((2, HH, HD, HH, M), pm.dtype)
    for h in range(HH):
        feat[:, h, :, h, :] = pm.T
    sel = np.zeros((128, HH, M), np.float16)
    for h in range(HH):
        sel[[h, HH + h], h, :] = 1
    low = np.zeros((128, 1), np.float32)
    low[64:] = 1
    arrays = {
        "x": x,
        "wk2": twice(qkv_w[D:2 * D]).transpose(2, 0, 1),
        "wq2": twice(qkv_w[0:D]).transpose(2, 0, 1),
        "wvg": np.concatenate([qkv_w[2 * D:].T, wg], axis=1),
        "bk2": twice(qkv_b[D:2 * D])[:, :, 0].T,
        "bq2": twice(qkv_b[0:D])[:, :, 0].T,
        "bv": np.broadcast_to(qkv_b[2 * D:], (128, D)),
        "wp": proj_w.T,
        "bp": np.broadcast_to(proj_b, (128, D)),
        "feat": feat.reshape(128, HH * M),
        "sel": sel.reshape(128, HH * M),
        "split": low,
        "ident": np.eye(128, dtype=np.float32),
        "w1": w1.transpose(1, 0, 2),
        "b1": b1.reshape(E * HF // 128, 128).T,
        "w2": w2.reshape(E * HF // 128, 128, D).transpose(1, 0, 2),
        "b2": np.broadcast_to(b2, (128, E, D)),
        "lanes": np.broadcast_to(np.arange(E, 0, -1, dtype=np.float32), (128, E)),
    }
    nc = bacc.Bacc("TRN2", target_bir_lowering=False, num_devices=1)
    ins, aps = {}, []
    for name, v in arrays.items():
        v = np.ascontiguousarray(v)
        ins[f"in_{name}"] = v
        aps.append(nc.dram_tensor(f"in_{name}", v.shape, mybir.dt.from_np(v.dtype), kind="ExternalInput").ap())
    out = nc.dram_tensor("out_0", x.shape, mybir.dt.from_np(x.dtype), kind="ExternalOutput").ap()
    favor_moe_block(nc, *aps, out)
    r = run_bass_kernel_spmd(nc, [ins], core_ids=[0])
    return r.results[0]["out_0"]
```

```python
import concourse.bass as bass
from concourse import mybir
from collections import namedtuple
from contextlib import ExitStack

F32 = mybir.dt.float32
F16 = mybir.dt.float16
I32 = mybir.dt.int32
U32 = mybir.dt.uint32
ALU = mybir.AluOpType
ACT = mybir.ActivationFunctionType
AX = mybir.AxisListType


def favor_moe_block(nc, x, wk2, wq2, wvg, bk2, bq2, bv, wp, bp, feat, sel, split, ident, w1, b1, w2, b2, lanes, tile_no, below, ones, out):
    NB, S, D = x.shape
    P = 128
    BT = 4
    BW = BT * P
    NBLK = NB * S // BW
    PER = S // BW
    H, M = 16, 64
    HD = D // H
    NH = 2
    HH = H // NH
    FW = HH * M
    NP = H // 2
    PH = NP // NH
    UN = NH * BT
    C = HD + 1
    E, HF = w1.shape[1], w1.shape[2]
    CH = E * HF // P
    HC = HF // P
    K = 2
    TR = 256
    TT = TR // P
    TILES = NB * S * K // TR + E - 1
    REGION = NB * S + TR
    SPARE = (E - 1) * TR
    ROWS = E * REGION + SPARE
    W_SCALE = 2.0 ** 6
    EPS = 1e-6
    LIFT = 14
    LIFT_BIAS = LIFT * 0.6931471805599453
    FEAT_EPS = EPS * M ** 0.5 * 2.0 ** LIFT
    KV_SCALE = 2.0 ** -15
    DEN_EPS = EPS * M * 2.0 ** (2 * LIFT) * KV_SCALE

    xv = x.rearrange("b (k t p) d -> p (b k) t d", p=P, t=BT)
    ov = out.rearrange("b (k t p) d -> p (b k) t d", p=P, t=BT)

    with ExitStack() as ctx:
        def sb(name, shape, dt=F32):
            return ctx.enter_context(nc.sbuf_tensor(name, shape, dt))

        def sem(name):
            return ctx.enter_context(nc.semaphore(name))

        wk_sb, wq_sb = sb("wk_sb", [P, NH, P]), sb("wq_sb", [P, NH, P])
        wvg_sb = sb("wvg_sb", [P, D + E])
        bk_sb, bq_sb = sb("bk_sb", [P, NH]), sb("bq_sb", [P, NH])
        bv_sb, bp_sb = sb("bv_sb", [P, D]), sb("bp_sb", [P, D])
        wp_sb = sb("wp_sb", [P, D])
        feat_sb = sb("feat_sb", [P, FW])
        feat_hi, feat_lo = sb("feat_hi", [P, FW], F16), sb("feat_lo", [P, FW], F16)
        sel_sb = sb("sel_sb", [P, FW], F16)
        low_rows = sb("low_rows", [P, 1])
        bk_low, bq_low = sb("bk_low", [P, NH]), sb("bq_low", [P, NH])
        ident_sb = sb("ident_sb", [P, P])
        ident16 = sb("ident16", [P, P], F16)
        lift_sb = sb("lift_sb", [P, 1])
        half_pow = sb("half_pow", [P, BT])
        w1_sb = sb("w1_sb", [P, E, HF])
        w1_hi, w1_lo = sb("w1_hi", [P, E, HF], F16), sb("w1_lo", [P, E, HF], F16)
        b1_sb = sb("b1_sb", [P, CH])
        w2_sb = sb("w2_sb", [P, CH, D])
        b2_sb = sb("b2_sb", [P, E, D])
        lanes_sb = sb("lanes_sb", [P, E])
        tile_no_sb = sb("tile_no_sb", [P, TILES])
        below_sb, ones_sb = sb("below_sb", [P, P], F16), sb("ones_sb", [P, P], F16)
        zeros = sb("zeros", [P, P])
        acc = sb("acc", [P, NBLK, BW])
        xnT_all = sb("xnT_all", [P, NBLK, BW])
        top_all = sb("top_all", [P, K, NBLK * BT])
        scores = sb("scores", [P, K, NBLK * BT])
        slots_all = sb("slots_all", [P, NBLK, K * BT])
        y_slots = sb("y_slots", [P, NBLK, K * BT], U32)
        kv_all = sb("kv_all", [P, NB, NP, 2, 2 * C], F16)
        xb = sb("xb", [P, PER, BT, D])
        xn = sb("xn", [P, PER, BT, D])
        stat, mv = sb("stat", [P, BT, 6]), sb("mv", [P, BT, 2])
        veps, rstd = sb("veps", [P, BT]), sb("rstd", [P, BT])
        xnT = sb("xnT", [P, PER, BW])
        part_hi = sb("part_hi", [P, NH, BW], F16)
        stack = sb("stack", [P, PER, NH, BW], F16)
        v32 = sb("v32", [P, 2, 2 * P])
        v16 = sb("v16", [P, PER, BT, NP, 2, 2 * C], F16)
        NE = 8
        e_hi = sb("e_hi", [P, NE, FW], F16)
        e_32 = sb("e_32", [P, NE, FW])
        e_lo = sb("e_lo", [P, NE, FW], F16)
        NM = 4
        mx = sb("mx", [P, NM, HH])
        mx16 = sb("mx16", [P, NM, P], F16)
        mxT = sb("mxT", [P, 2, P], F16)
        mxT_q = sb("mxT_q", [P, PER, NH, BW], F16)
        kv_low, kv32 = sb("kv_low", [P, NP, 2 * C]), sb("kv32", [P, NP, 2 * C])
        kv_now = sb("kv_now", [P, NP, 2, 2 * C], F16)
        den = sb("den", [P, 2, 2, H])
        attn = sb("attn", [P, BT, D])
        attnT = sb("attnT", [P, BW])
        res = sb("res", [P, PER, BW])
        lg = sb("lg", [P, PER, BT, E])
        lg2, tmp2, tmp, key = sb("lg2", [P, BT, E]), sb("tmp2", [P, BT, E]), sb("tmp", [P, K, BT, E]), sb("key", [P, BT])
        one = sb("one", [P, K, BT, E])
        chosen = sb("chosen", [P, BT + 1, E], F16)
        rank = sb("rank", [P, PER, BT + 1, E])
        slot32, slot = sb("slot32", [P, K * BT]), sb("slot", [P, PER, K * BT], U32)
        cnt, steps_of, over = sb("cnt", [P, E]), sb("steps_of", [P, E]), sb("over", [P, E])
        tab = sb("tab", [P, 2 * 72 + E], I32)
        NX = 4
        x_tile = sb("x_tile", [P, NX, TT, D])
        xt_hi, xt_lo = sb("xt_hi", [P, 2, TR], F16), sb("xt_lo", [P, 2, TR], F16)
        hid = [sb("hid0", [P, 2, TR]), sb("hid1", [P, 2, TR])]
        y_tile = sb("y_tile", [P, NX, TT, D])
        y_got = sb("y_got", [P, PER, K * BT, D])
        moe = xb[:, 0]
        x_rows = nc.dram_tensor("x_rows", [ROWS, D], F32, kind="Internal").ap()
        y_rows = nc.dram_tensor("y_rows", [TILES * TR, D], F32, kind="Internal").ap()
        bank = [ctx.enter_context(nc.psum_tensor(f"bank{n}", [P, 512], F32)) for n in range(8)]

        block = ctx.enter_context(nc.Block())
        w_in, s_const, pow_const = sem("w_in"), sem("s_const"), sem("pow_const")
        x_in = [sem(f"x_in{k}") for k in range(PER)]
        stats_done, rstd_done, xn_ready, acc_ready = sem("stats_done"), sem("rstd_done"), sem("xn_ready"), sem("acc_ready")
        xT_done, xT_kept, kT_done, khi_done, kst_ready = sem("xT_done"), sem("xT_kept"), sem("kT_done"), sem("khi_done"), sem("kst_ready")
        v_done, v_taken, vhi_done, vlo_done = sem("v_done"), sem("v_taken"), sem("vhi_done"), sem("vlo_done")
        feat_done, mx_ready, mxT_done, mxT_ready, shifted = sem("feat_done"), sem("mx_ready"), sem("mxT_done"), sem("mxT_ready"), sem("shifted")
        exp_done, dp_free, elo_ready, e_free = sem("exp_done"), sem("dp_free"), sem("elo_ready"), sem("e_free")
        kvlow_done, kv_taken, kvhi_done, kv_split = sem("kvlow_done"), sem("kv_taken"), sem("kvhi_done"), sem("kv_split")
        dve_step = sem("dve_step")
        ln_step, mx_step, qmx_step, nrm_step, mxh_step, qmxh_step = [sem(n) for n in ("ln_step", "mx_step", "qmx_step", "nrm_step", "mxh_step", "qmxh_step")]
        act_step = sem("act_step")
        routed, e2_done = sem("routed"), sem("e2_done")
        choice_step, chosen_ready, rank_done, rank_ready, scattered = sem("choice_step"), sem("chosen_ready"), sem("rank_done"), sem("rank_ready"), [sem(f"scattered{k}") for k in range(PER)]
        tab_ready, zeroed = sem("tab_ready"), sem("zeroed")
        tile_in, y_stored = [sem(f"tile_in{n}") for n in range(4)], [sem(f"y_stored{n}") for n in range(4)]
        tile_turned, thi_done, tlo_done = sem("tile_turned"), sem("thi_done"), sem("tlo_done")
        z_done, h_ready = [sem("z0_done"), sem("z1_done")], [sem("h0_ready"), sem("h1_ready")]
        y_done, y_kept, whi_done, w_ready = sem("y_done"), sem("y_kept"), sem("whi_done"), sem("w_ready")
        slots_kept, y_slots_ready, slot_step, slot_part, slot_ready, gathered, moe_half, moe_ready = sem("slots_kept"), sem("y_slots_ready"), sem("slot_step"), sem("slot_part"), sem("slot_ready"), [sem(f"gathered{k}") for k in range(PER)], sem("moe_half"), sem("moe_ready")
        qT_done, qhi_done, qst_ready = sem("qT_done"), sem("qhi_done"), sem("qst_ready")
        qf_done, qmx_ready, qmxT_done, qmxT_ready = sem("qf_done"), sem("qmx_ready"), sem("qmxT_done"), sem("qmxT_ready")
        qs_done, qexp_done, qlo_ready, qe_free, qs_free = sem("qs_done"), sem("qexp_done"), sem("qlo_ready"), sem("qe_free"), sem("qs_free")
        kv_now_ready, attn_ready, aT_done, aT_ready, proj_done, res_ready = (
            sem("kv_now_ready"), sem("attn_ready"), sem("aT_done"), sem("aT_ready"), sem("proj_done"), sem("res_ready"))
        out_done = [sem(f"out_done{k}") for k in range(PER)]

        dp = bank[0:4]
        xk, vb, mt, kvb = bank[4], bank[5], bank[6], bank[7]
        mt16 = mt[:, 0:64].bitcast(F16)
        kv_ps = kvb[:, 0:NP * 4 * C].rearrange("p (n s c) -> p n s c", n=NP, s=2)
        tm, fm, ob = bank[0:2], bank[2:4], bank[4:6]
        qb = bank[7]
        rank_ps = vb[:, 2 * (D + E):2 * (D + E) + (BT + 1) * E]
        xt_ps, z_ps, y_ps = bank[0:2], [bank[2:4], bank[6:8]], bank[4:6]

        def turned(b, s):
            if s >= QTURN_LAG:
                return (after(b), s - QTURN_LAG) if after(b) else None
            return None if type(b.n) is int and b.n == 0 else (b, s - QTURN_LAG + UN)

        TURN_LAG, EXP_LAG, LOW_LAG, KV_LAG = 2, 3, 5, 6
        XT_STEP, KT_STEP = 4, 5
        RANK_STEP = 3
        QTURN_LAG, QLOW_LAG, OUT_LAG = 2, 1, 3
        Q1_STEP, AT_STEP, PROJ_STEP, Q0_STEP = 0, 4, 5, 6
        WAITS_W = 16 * 20

        def load_weights(eng):
            for dst, src in ((wk_sb[:], wk2), (wvg_sb[:], wvg), (bk_sb[:], bk2), (low_rows[:], split),
                             (feat_sb[:], feat), (sel_sb[:], sel), (ident_sb[:], ident), (bv_sb[:], bv),
                             (bp_sb[:], bp), (wq_sb[:], wq2), (bq_sb[:], bq2), (wp_sb[:], wp),
                             (w1_sb[:], w1), (b1_sb[:], b1), (w2_sb[:], w2), (b2_sb[:], b2), (lanes_sb[:], lanes),
                             (tile_no_sb[:], tile_no), (below_sb[:], below), (ones_sb[:], ones)):
                eng.dma_start(dst, src).then_inc(w_in, 16)

        Block = namedtuple("Block", "n k batch")

        def after(b, ahead=1):
            for _ in range(ahead):
                b = Block(b.n + 1, (b.k + 1) % PER, b.batch + 1 if b.k == PER - 1 else b.batch)
            return None if type(b.n) is int and b.n >= NBLK else b

        def over_blocks(eng, body, ahead):
            body(Block(0, 0, 0))
            pairs = (NBLK - 1 - ahead) // PER
            with eng.Fori(0, pairs) as i:
                body(Block(PER * i + 1, 1, i))
                body(Block(PER * i + 2, 0, i + 1))
            for n in range(PER * pairs + 1, NBLK):
                body(Block(n, n % PER, n // PER))

        def step_of(b, s, lag, units):
            u = s - lag
            if u >= 0:
                return b, u
            if type(b.n) is int and b.n == 0:
                return None
            return Block(b.n - 1, (b.k + 1) % PER, b.batch if b.k else b.batch - 1), u + units

        ONE = 1
        from_one = [kv_taken, mxT_ready, kv_split, attn_ready, aT_done, res_ready] + out_done

        Tile = namedtuple("Tile", "n g i")

        def tile(n):
            return Tile(n, n // NX, n % NX)

        def later(j, by):
            if type(j.n) is int:
                return tile(j.n + by) if j.n + by < TILES else None
            return Tile(j.n + by, j.g + (j.i + by) // NX, (j.i + by) % NX)

        def over_tiles(eng, body, ahead):
            groups = (TILES - ahead) // NX
            for n in range(NX):
                body(tile(n))
            with eng.Fori(1, groups) as g:
                for i in range(NX):
                    body(Tile(NX * g + i, g, i))
            for n in range(NX * groups, TILES):
                body(tile(n))

        def expert_of(eng, j):
            return eng.value_load(tab[0:1, bass.ds(j.n, 1)], min_val=0, max_val=E - 1)

        def row_of(eng, j):
            return eng.value_load(tab[0:1, bass.ds(j.n + 72, 1)], min_val=0, max_val=ROWS - TR)

        @block.sync
        def _(sp):
            for s in from_one:
                nc.sync.sem_inc(s, ONE)
            for k in range(PER):
                sp.dma_start(xb[:, k], xv[:, k]).then_inc(x_in[k], 16)
            load_weights(sp)
            sp.wait_ge(s_const, 2)
            for n in range(SPARE // P):
                sp.dma_start(x_rows[E * REGION + n * P:E * REGION + (n + 1) * P], zeros[:]).then_inc(zeroed, 16)
            with sp.Fori(1, NB) as i:
                for k in range(PER):
                    sp.wait_ge(xn_ready, PER * i + k - PER + 1)
                    sp.wait_ge(acc_ready, PER * i + k - PER + 1)
                    sp.dma_start(xb[:, k], xv[:, bass.ds(PER * i + k, 1)].rearrange("p o t d -> p (o t) d")).then_inc(x_in[k], 16)
            sp.wait_ge(tab_ready, 1)
            for e in range(E):
                row = sp.value_load(tab[0:1, 144 + e:145 + e], min_val=0, max_val=ROWS - TR)
                for t in range(TT):
                    sp.dma_start(x_rows[bass.ds(row + t * P, P)], zeros[:]).then_inc(zeroed, 16)
            sp.wait_ge(zeroed, 16 * (SPARE // P + E * TT))
            for k in range(PER):
                sp.wait_ge(scattered[k], 16 * K * BT * NB)

            def rows(ap, row):
                return ap[bass.ds(row, TR)].rearrange("(t p) d -> p t d", p=P)

            def load_tile(j):
                row = row_of(sp, j)
                if type(j.n) is not int or j.n >= NX:
                    sp.wait_ge(tile_turned, j.n - NX + 1)
                sp.dma_start(x_tile[:, j.i], rows(x_rows, row)).then_inc(tile_in[j.i], 16)

            def tile_body(j):
                if later(j, NX):
                    load_tile(later(j, NX))
                sp.wait_ge(y_kept, j.n + 1)
                sp.dma_start(rows(y_rows, TR * j.n), y_tile[:, j.i]).then_inc(y_stored[j.i], 16)

            for n in range(NX):
                load_tile(tile(n))
            over_tiles(sp, tile_body, NX)
            with sp.Fori(0, NB) as i:
                for k in range(PER):
                    sp.wait_ge(res_ready, ONE + PER * i + k + 1)
                    sp.dma_start(ov[:, bass.ds(PER * i + k, 1)].rearrange("p o t d -> p (o t) d"),
                                 res[:, k].rearrange("p (t d) -> p t d", t=BT)).then_inc(out_done[k], 16)
            for k in range(PER):
                sp.wait_ge(out_done[k], ONE + 16 * NB)

        @block.gpsimd
        def _(pool):
            nc.gpsimd.memset(half_pow[:], -0.5).then_inc(pow_const, 1)
            pool.wait_ge(pow_const, 1)
            pool.wait_ge(s_const, 2)
            pool.wait_ge(w_in, WAITS_W)

            def rstds(b):
                pool.wait_ge(stats_done, b.n + 1)
                nc.gpsimd.tensor_tensor(out=rstd[:], in0=veps[:], in1=half_pow[:], op=ALU.pow).then_inc(rstd_done, 1)

            def residual(b):
                pool.wait_ge(x_in[b.k], 16 * b.batch + 16)
                nc.gpsimd.tensor_tensor(out=acc[:, bass.ds(b.n, 1)].rearrange("p o (t d) -> p (o t) d", d=D), in0=xb[:, b.k],
                                        in1=bp_sb[:].unsqueeze(1).to_broadcast([P, BT, D]), op=ALU.add).then_inc(acc_ready, 1)

            def values_low(b, j):
                pool.wait_ge(vhi_done, 2 * b.n + j + 1)
                d = v16[:, b.k, 2 * j:2 * j + 2].rearrange("p t n s (h c) -> p (t n) s h c", h=2)
                nc.gpsimd.tensor_tensor(out=d[:, :, 1, :, 0:HD], in0=v32[:, j].rearrange("p (n h c) -> p n h c", h=2, c=HD),
                                        in1=d[:, :, 0, :, 0:HD], op=ALU.subtract).then_inc(vlo_done, 1)

            def dispatch(b):
                pool.wait_ge(slot_ready, b.n + 1)
                nc.gpsimd.tensor_copy(slots_all[:, bass.ds(b.n, 1)].rearrange("p o n -> p (o n)"), slot[:, b.k]).then_inc(slots_kept, 1)
                for t in range(BT):
                    for r in range(K):
                        pool.indirect_dma_start(x_rows[:, :], bass.IndirectOffsetOnAxis(ap=slot[:, b.k, r * BT + t:r * BT + t + 1], axis=0),
                                                xn[:, b.k, t], None).then_inc(scattered[b.k], 16)

            def body(b):
                nb = after(b)
                if nb:
                    rstds(nb)
                    residual(nb)
                dispatch(b)
                if nb:
                    for j in range(2):
                        values_low(nb, j)

            z = Block(0, 0, 0)
            rstds(z)
            residual(z)
            for j in range(2):
                values_low(z, j)
            over_blocks(pool, body, 1)

            for n in range(NX):
                pool.wait_ge(y_stored[n], 16 * len(range(n, TILES, NX)))

            def slots_of(b):
                nc.gpsimd.tensor_copy(slot[:, b.k], y_slots[:, bass.ds(b.n, 1)].rearrange("p o n -> p (o n)")).then_inc(slot_step, 1)

            def gather(b):
                pool.wait_ge(slot_step, b.n + 1)
                if not (type(b.n) is int and b.n < 2):
                    pool.wait_ge(moe_ready, b.n - 1)
                if after(b):
                    if not (type(b.n) is int and b.n == 0):
                        pool.wait_ge(gathered[1 - b.k], 16 * K * BT * after(b).batch)
                    slots_of(after(b))
                for n in range(K * BT):
                    pool.indirect_dma_start(y_got[:, b.k, n], None, y_rows[:, :],
                                            bass.IndirectOffsetOnAxis(ap=slot[:, b.k, n:n + 1], axis=0)).then_inc(gathered[b.k], 16)

            pool.wait_ge(y_slots_ready, 1)
            slots_of(z)
            over_blocks(pool, gather, 1)

        @block.scalar
        def _(act):
            nc.scalar.sem_inc(dp_free, 4)
            act.wait_ge(w_in, WAITS_W)
            act.wait_ge(s_const, 2)

            def keep_xT(b):
                act.wait_ge(xT_done, b.n + 1)
                nc.scalar.activation(xnT[:, b.k], xk[:, :], ACT.Copy)
                nc.scalar.activation(xnT_all[:, bass.ds(b.n, 1)].rearrange("p o n -> p (o n)"), xk[:, :], ACT.Copy).then_inc(xT_kept, 1)

            def keys_high(b, a):
                act.wait_ge(kT_done, NH * b.n + a + 1)
                nc.scalar.activation(part_hi[:, a], xk[:, :], ACT.Identity, scale=low_rows[:, 0:1],
                                     bias=bk_low[:, a:a + 1]).then_inc(khi_done, 1)

            def values_high(b, j):
                act.wait_ge(v_taken, 2 * b.n + j + 1)
                d = v16[:, b.k, 2 * j:2 * j + 2].rearrange("p t n s (h c) -> p (t n) s h c", h=2)
                nc.scalar.activation(d[:, :, 0, :, 0:HD], v32[:, j].rearrange("p (n h c) -> p n h c", h=2, c=HD),
                                     ACT.Copy).then_inc(vhi_done, 1)

            def keep_key_max(b, u):
                act.wait_ge(mxT_done, UN * b.n + u + 1)
                nc.scalar.activation(mxT[:, u % 2], mt16, ACT.Copy).then_inc(mxT_ready, 1)

            def key_exps(b, u):
                act.wait_ge(shifted, UN * b.n + u + 1)
                act.wait_ge(e_free, UN * b.n + u + 1)
                nc.scalar.activation(e_hi[:, u % NE], dp[u % 4][:, :], ACT.Exp, bias=lift_sb[:, 0:1])
                nc.scalar.activation(e_32[:, u % NE], dp[u % 4][:, :], ACT.Exp, bias=lift_sb[:, 0:1])\
                    .then_inc(dp_free, 1)

            def batch_high(batch):
                act.wait_ge(e_free, NE + UN * PER * (batch + 1))
                nc.scalar.activation(kv_low[:], kv_ps[:, :, 1, :], ACT.Copy, scale=KV_SCALE).then_inc(kvlow_done, 1)
                act.wait_ge(kv_taken, ONE + batch + 1)
                kd = kv_all[:, bass.ds(batch, 1)].rearrange("p o n s c -> p (o n) s c")
                for g in range(2):
                    r, c = slice(64 * g, 64 * g + 64), slice(C * g, C * g + C)
                    nc.scalar.activation(kd[r, :, 0, c], kv32[r, :, c], ACT.Copy).then_inc(kvhi_done, 1)

            def body(b):
                nb = after(b)
                for s in range(UN):
                    if s == KV_LAG and (at := step_of(b, s, KV_LAG + 1, UN)) and b.k == 0:
                        batch_high(at[0].batch)
                    if at := step_of(b, s, TURN_LAG, UN):
                        keep_key_max(*at)
                    if at := step_of(b, s, EXP_LAG, UN):
                        key_exps(*at)
                    if nb and s == XT_STEP:
                        keep_xT(nb)
                    if nb and s == KT_STEP:
                        keys_high(nb, 0)
                    if nb and s == KT_STEP + 1:
                        keys_high(nb, 1)
                    if nb and s == UN - 1:
                        values_high(nb, 0)
                        values_high(nb, 1)

            keep_xT(Block(0, 0, 0))
            keys_high(Block(0, 0, 0), 0)
            keys_high(Block(0, 0, 0), 1)
            values_high(Block(0, 0, 0), 0)
            values_high(Block(0, 0, 0), 1)
            over_blocks(act, body, 1)
            end = Block(NBLK - 1, PER - 1, NB - 1)
            for s in range(EXP_LAG):
                if s < TURN_LAG:
                    keep_key_max(end, UN - TURN_LAG + s)
                key_exps(end, UN - EXP_LAG + s)
            batch_high(NB - 1)

            act.wait_ge(routed, 1)
            nc.scalar.activation(scores[:, 1], scores[:, 0], ACT.Exp).then_inc(e2_done, 1)

            nc.scalar.sem_inc(qs_free, 2)
            def queries_high(b, a):
                act.wait_ge(qT_done, NH * b.n + a + 1)
                nc.scalar.activation(part_hi[:, a], qb[:, :], ACT.Identity, scale=low_rows[:, 0:1],
                                     bias=bq_low[:, a:a + 1]).then_inc(qhi_done, 1)

            def keep_max(b, u):
                act.wait_ge(qmxT_done, UN * b.n + u + 1)
                a, t = divmod(u, BT)
                nc.scalar.activation(mxT_q[:, b.k, a, t * P:(t + 1) * P], mt16, ACT.Copy).then_inc(qmxT_ready, 1)

            def query_exps(b, j):
                act.wait_ge(qs_done, NP * b.n + j + 1)
                act.wait_ge(qe_free, NP * b.n + j + 1)
                nc.scalar.activation(e_hi[:, j % NE], fm[j % 2][:, :], ACT.Exp, bias=lift_sb[:, 0:1])
                nc.scalar.activation(e_32[:, j % NE], fm[j % 2][:, :], ACT.Exp, bias=lift_sb[:, 0:1])\
                    .then_inc(qs_free, 1)

            def keep_aT(b):
                act.wait_ge(aT_done, ONE + b.n + 1)
                nc.scalar.activation(attnT[:], qb[:, :], ACT.Copy).then_inc(aT_ready, 1)

            def qbody(b):
                nb, nnb = after(b), after(b, 2)
                for s in range(NP):
                    if nb and s == Q1_STEP:
                        queries_high(nb, 1)
                    query_exps(b, s)
                    if at := turned(b, s):
                        keep_max(*at)
                    if s == AT_STEP and step_of(b, s, UN, UN):
                        keep_aT(step_of(b, s, UN, UN)[0])
                    if nnb and s == Q0_STEP:
                        queries_high(nnb, 0)

            z = Block(0, 0, 0)
            queries_high(z, 0)
            queries_high(z, 1)
            for u in range(UN):
                keep_max(z, u)
            queries_high(after(z), 0)

            nc.scalar.activation(w1_hi[:], w1_sb[:], ACT.Copy, scale=W_SCALE).then_inc(whi_done, 1)
            nc.scalar.activation(b1_sb[:], b1_sb[:], ACT.Copy, scale=W_SCALE)
            nc.scalar.activation(w2_sb[:], w2_sb[:], ACT.Copy, scale=1 / W_SCALE).then_inc(w_ready, 1)
            act.wait_ge(w_ready, 2)

            def tile_high(j):
                act.wait_ge(tile_turned, j.n + 1)
                if type(j.n) is not int or j.n >= 2:
                    act.wait_ge(z_done[1], j.n - 1)
                nc.scalar.activation(xt_hi[:, j.i % 2], xt_ps[j.i % 2][:, 0:TR], ACT.Copy).then_inc(thi_done, 1)

            def hidden_first(j):
                e = expert_of(act, j)
                act.wait_ge(z_done[0], j.n + 1)
                if type(j.n) is not int or j.n >= 2:
                    act.wait_ge(y_done, j.n - 1)
                nc.scalar.activation(hid[0][:, j.i % 2], z_ps[0][j.i % 2][:, 0:TR], ACT.Relu,
                                     bias=b1_sb[:, bass.ds(HC * e, 1)]).then_inc(h_ready[0], 1)

            def tile_body(j):
                if later(j, 2):
                    tile_high(later(j, 2))
                if later(j, 1):
                    hidden_first(later(j, 1))

            tile_high(tile(0))
            tile_high(tile(1))
            hidden_first(tile(0))
            over_tiles(act, tile_body, 2)

            over_blocks(act, qbody, 2)
            keep_aT(Block(NBLK - 1, PER - 1, NB - 1))

        @block.vector
        def _(dve):
            steps = [0]

            nc.vector.memset(lift_sb[:], LIFT_BIAS)
            nc.vector.memset(mx16[:], 0.0)
            nc.vector.memset(kv_all[:], 0.0)
            nc.vector.memset(zeros[:], 0.0)
            nc.vector.memset(chosen[:], 0.0)
            nc.vector.memset(v16[:, :, :, :, 1], 0.0)
            nc.vector.memset(v16[:, :, :, :, 0], 1.0).then_inc(s_const, 1)
            dve.wait_ge(w_in, WAITS_W)
            nc.vector.tensor_copy(ident16[:], ident_sb[:])
            nc.vector.tensor_scalar(out=rank[:, PER - 1, BT], in0=lanes_sb[:], scalar1=-float(REGION), scalar2=float(E * REGION),
                                    op0=ALU.mult, op1=ALU.add)
            nc.vector.tensor_tensor(out=bk_low[:], in0=bk_sb[:], in1=low_rows[:].to_broadcast([P, NH]), op=ALU.mult)
            nc.vector.tensor_tensor(out=bq_low[:], in0=bq_sb[:], in1=low_rows[:].to_broadcast([P, NH]), op=ALU.mult)
            nc.vector.tensor_scalar(out=e_32[:, 0], in0=feat_sb[:], scalar1=float(HD) ** -0.5, scalar2=None, op0=ALU.mult).then_inc(dve_step, 1)
            dve.wait_ge(dve_step, 1)
            nc.vector.tensor_copy(feat_hi[:], e_32[:, 0]).then_inc(dve_step, 1)
            dve.wait_ge(dve_step, 2)
            nc.vector.tensor_tensor(out=feat_lo[:], in0=e_32[:, 0], in1=feat_hi[:], op=ALU.subtract).then_inc(s_const, 1)

            SETUP = 2

            def stats(b):
                dve.wait_ge(x_in[b.k], 16 * b.batch + 16)
                if not (type(b.n) is int and b.n == 0):
                    dve.wait_ge(rstd_done, b.n)
                for t in range(BT):
                    last = nc.vector.bn_stats(out=stat[:, t], in_=xb[:, b.k, t])
                last.then_inc(ln_step, 1)

            def stats_seen(b):
                dve.wait_ge(ln_step, 2 * b.n + 1)

            def means(b):
                for t in range(BT):
                    last = nc.vector.bn_aggr(out=mv[:, t], in_=stat[:, t])
                last.then_inc(ln_step, 1)

            def variance(b):
                dve.wait_ge(ln_step, 2 * b.n + 2)
                nc.vector.tensor_scalar(out=veps[:], in0=mv[:, :, 1], scalar1=1e-5, scalar2=None, op0=ALU.add).then_inc(stats_done, 1)

            def normalise(b):
                dve.wait_ge(rstd_done, b.n + 1)
                if not (type(b.n) is int and b.n < 2):
                    dve.wait_ge(scattered[b.k], 16 * K * BT * b.batch)
                for t in range(BT):
                    last = nc.vector.tensor_scalar(out=xn[:, b.k, t], in0=xb[:, b.k, t], scalar1=mv[:, t, 0:1],
                                                   scalar2=rstd[:, t:t + 1], op0=ALU.subtract, op1=ALU.mult)
                last.then_inc(xn_ready, 1)

            def kstack(b, a):
                dve.wait_ge(khi_done, NH * b.n + a + 1)
                nc.vector.scalar_tensor_tensor(out=stack[:, b.k, a], in0=xk[:, :], scalar=bk_sb[:, a:a + 1], in1=part_hi[:, a],
                                               op0=ALU.add, op1=ALU.subtract).then_inc(kst_ready, 1)

            def values(b, j):
                dve.wait_ge(v_done, 2 * b.n + j + 1)
                if not (type(b.n) is int and b.n == 0):
                    dve.wait_ge(vlo_done, 2 * b.n + j - 1)
                vp = vb[:, 0:2 * (D + E)].rearrange("p (t c) -> p t c", t=2)
                nc.vector.tensor_tensor(out=v32[:, j].rearrange("p (t c) -> p t c", t=2), in0=vp[:, :, 0:D],
                                        in1=bv_sb[:].unsqueeze(1).to_broadcast([P, 2, D]), op=ALU.add)
                nc.vector.tensor_copy(lg[:, b.k, 2 * j:2 * j + 2], vp[:, :, D:D + E]).then_inc(v_taken, 1)

            def maximum(psum, done, b, u, own):
                dve.wait_ge(done, UN * b.n + u + 1)
                nc.vector.tensor_reduce(out=mx[:, u % NM], in_=psum[:, :].rearrange("p (h m) -> p h m", h=HH), axis=AX.X,
                                        op=ALU.max, negate=True).then_inc(own[0], 1)

            def max_high(b, u, own):
                dve.wait_ge(own[0], UN * b.n + u + 1)
                nc.vector.tensor_copy(mx16[:, u % NM, 0:HH], mx[:, u % NM]).then_inc(own[1], 1)

            def max_low(b, u, own, ready):
                dve.wait_ge(own[1], UN * b.n + u + 1)
                nc.vector.tensor_tensor(out=mx16[:, u % NM, HH:2 * HH], in0=mx[:, u % NM], in1=mx16[:, u % NM, 0:HH],
                                        op=ALU.subtract).then_inc(ready, 1)

            def low_part(u, exps, count, ready):
                dve.wait_ge(exps, count)
                nc.vector.scalar_tensor_tensor(out=e_lo[:, u % NE], in0=e_32[:, u % NE], scalar=FEAT_EPS, in1=e_hi[:, u % NE],
                                               op0=ALU.add, op1=ALU.subtract).then_inc(ready, 1)

            def key_low(b, u):
                low_part(u, dp_free, 4 + UN * b.n + u + 1, elo_ready)

            def batch_low(batch):
                dve.wait_ge(kv_split, ONE + 2 * batch)
                dve.wait_ge(kvlow_done, batch + 1)
                nc.vector.scalar_tensor_tensor(out=kv32[:], in0=kv_ps[:, :, 0, :], scalar=KV_SCALE, in1=kv_low[:],
                                               op0=ALU.mult, op1=ALU.add).then_inc(kv_taken, 1)
                kd = kv_all[:, bass.ds(batch, 1)].rearrange("p o n s c -> p (o n) s c")
                dve.wait_ge(kvhi_done, 2 * batch + 2)
                for g in range(2):
                    r, c = slice(64 * g, 64 * g + 64), slice(C * g, C * g + C)
                    nc.vector.tensor_tensor(out=kd[r, :, 1, c], in0=kv32[r, :, c], in1=kd[r, :, 0, c],
                                            op=ALU.subtract).then_inc(kv_split, 1)

            bc = lambda v: v.unsqueeze(2).to_broadcast([P, BT, E])
            lanes_bc = lanes_sb[:].unsqueeze(1).to_broadcast([P, BT, E])
            CHOOSE = 12

            def choose(b, n):
                r, part = divmod(n, 6)
                if n == 0:
                    dve.wait_ge(v_taken, 2 * b.n + 2)
                else:
                    dve.wait_ge(choice_step, (CHOOSE - 1) * b.n + n)
                if n == 4 and not (type(b.n) is int and b.n == 0):
                    dve.wait_ge(slot_ready, b.n)
                src = lg2[:] if r else lg[:, b.k]
                if part == 0:
                    op = nc.vector.tensor_reduce(out=top_all[:, r, bass.ds(BT * b.n, BT)], in_=src, axis=AX.X, op=ALU.max)
                elif part == 1:
                    op = nc.vector.tensor_tensor(out=tmp2[:], in0=src, in1=bc(top_all[:, r, bass.ds(BT * b.n, BT)]), op=ALU.is_equal)
                elif part == 2:
                    op = nc.vector.tensor_tensor(out=tmp2[:], in0=tmp2[:], in1=lanes_bc, op=ALU.mult)
                elif part == 3:
                    op = nc.vector.tensor_reduce(out=key[:], in_=tmp2[:], axis=AX.X, op=ALU.max)
                elif part == 4:
                    op = nc.vector.tensor_tensor(out=one[:, r], in0=lanes_bc, in1=bc(key[:]), op=ALU.is_equal)
                elif r == 0:
                    op = nc.vector.scalar_tensor_tensor(out=lg2[:], in0=one[:, 0], scalar=-3e38, in1=src, op0=ALU.mult, op1=ALU.add)
                else:
                    op = nc.vector.tensor_tensor(out=chosen[:, 0:BT], in0=one[:, 0], in1=one[:, 1], op=ALU.add)
                op.then_inc(chosen_ready if n == CHOOSE - 1 else choice_step, 1)

            def ranks(b):
                dve.wait_ge(rank_done, b.n + 1)
                nc.vector.tensor_tensor(out=rank[:, b.k], in0=rank_ps.rearrange("p (t e) -> p t e", e=E),
                                        in1=rank[:, 1 - b.k, BT].unsqueeze(1).to_broadcast([P, BT + 1, E]), op=ALU.add).then_inc(rank_ready, 1)

            def slots(b, part):
                if part == 0:
                    dve.wait_ge(rank_ready, b.n + 1)
                    nc.vector.tensor_tensor(out=tmp[:], in0=one[:], in1=rank[:, b.k, 0:BT].unsqueeze(1).to_broadcast([P, K, BT, E]),
                                            op=ALU.mult).then_inc(slot_part, 1)
                elif part == 1:
                    dve.wait_ge(slot_part, 2 * b.n + 1)
                    nc.vector.tensor_reduce(out=slot32[:], in_=tmp[:].rearrange("p r t e -> p (r t) e"), axis=AX.X,
                                            op=ALU.add).then_inc(slot_part, 1)
                else:
                    dve.wait_ge(slot_part, 2 * b.n + 2)
                    if not (type(b.n) is int and b.n < 2):
                        dve.wait_ge(scattered[b.k], 16 * K * BT * b.batch)
                    nc.vector.tensor_copy(slot[:, b.k], slot32[:]).then_inc(slot_ready, 1)

            kown = (mx_step, mxh_step)

            def body(b):
                nb = after(b)
                for s in range(UN):
                    if at := step_of(b, s, 1, UN):
                        max_low(*at, kown, mx_ready)
                    if 4 * s < CHOOSE:
                        choose(b, 4 * s)
                    if s == RANK_STEP + 1:
                        slots(b, 0)
                    if at := step_of(b, s, LOW_LAG, UN):
                        key_low(*at)
                    if nb and s == 1:
                        stats_seen(nb)
                    if 4 * s < CHOOSE:
                        choose(b, 4 * s + 1)
                    if s == UN - 1 and nb:
                        values(nb, 0)
                    if nb and s == 1:
                        means(nb)
                    if s == RANK_STEP + 1:
                        slots(b, 1)
                    maximum(dp[s % 4], feat_done, b, s, kown)
                    if 4 * s < CHOOSE:
                        choose(b, 4 * s + 2)
                    if nb and s == 1:
                        variance(nb)
                    if s == KV_LAG and (at := step_of(b, s, KV_LAG + 1, UN)) and b.k == 0:
                        batch_low(at[0].batch)
                    if s == RANK_STEP + 1:
                        slots(b, 2)
                    max_high(b, s, kown)
                    if 4 * s < CHOOSE:
                        choose(b, 4 * s + 3)
                    if s == RANK_STEP:
                        ranks(b)
                    if nb and s == 0:
                        stats(nb)
                    if nb and s == XT_STEP - 1:
                        normalise(nb)
                    if nb and s == KT_STEP:
                        kstack(nb, 0)
                    if nb and s == KT_STEP + 1:
                        kstack(nb, 1)
                    if nb and s == UN - 1:
                        values(nb, 1)

            z = Block(0, 0, 0)
            stats(z)
            stats_seen(z)
            means(z)
            variance(z)
            normalise(z)
            kstack(z, 0)
            kstack(z, 1)
            values(z, 0)
            values(z, 1)
            over_blocks(dve, body, 1)
            end = Block(NBLK - 1, PER - 1, NB - 1)
            max_low(end, UN - 1, kown, mx_ready)
            for u in range(UN - LOW_LAG, UN):
                key_low(end, u)
            batch_low(NB - 1)

            n = [SETUP]

            def link(ins):
                n[0] += 1
                ins.then_inc(dve_step, 1)
                dve.wait_ge(dve_step, n[0])

            add_up = lambda out, in_: link(nc.vector.tensor_reduce(out=out, in_=in_, axis=AX.X, op=ALU.add))
            tt = lambda out, in0, in1, op: link(nc.vector.tensor_tensor(out=out, in0=in0, in1=in1, op=op))
            ts = lambda out, in0, a, op, b=None, op1=None: link(
                nc.vector.tensor_scalar(out=out, in0=in0, scalar1=a, scalar2=b, op0=op, **({"op1": op1} if op1 else {})))
            flat = e_32[:, 0:4].rearrange("p n w -> p (n w)")
            most = NB * S // TR
            full = flat[:, 0:E * most].rearrange("p (e k) -> p e k", k=most)
            sums = flat[:, 0:E * E].rearrange("p (o e) -> p o e", e=E)
            past = flat[:, 0:TILES * E].rearrange("p (j e) -> p j e", e=E)
            skips = flat[:, TILES * E:2 * TILES * E].rearrange("p (j e) -> p j e", e=E)
            first = flat[:, 2 * TILES * E:2 * TILES * E + TILES]
            rows = flat[:, 2 * TILES * E + TILES:2 * TILES * E + 2 * TILES]
            ends = rank[:, (NBLK - 1) % PER, BT]
            dve.wait_ge(elo_ready, NBLK * UN)
            dve.wait_ge(rank_ready, NBLK)
            nc.vector.tensor_copy(tab[:, 144:144 + E], ends)
            ts(cnt[:], lanes_sb[:], float(REGION), ALU.mult, -float(E * REGION), ALU.add)
            tt(cnt[:], cnt[:], ends, ALU.add)
            ts(cnt[:], cnt[:], 1.0 / TR, ALU.mult)
            tt(full, cnt[:].unsqueeze(2).to_broadcast([P, E, most]),
               tile_no_sb[:, 0:most].unsqueeze(1).to_broadcast([P, E, most]), ALU.is_gt)
            add_up(steps_of[:], full)
            tt(sums, lanes_sb[:].unsqueeze(1).to_broadcast([P, E, E]), lanes_sb[:].unsqueeze(2).to_broadcast([P, E, E]), ALU.is_ge)
            tt(sums, sums, steps_of[:].unsqueeze(1).to_broadcast([P, E, E]), ALU.mult)
            add_up(over[:], sums)
            ts(steps_of[:], steps_of[:], -float(TR), ALU.mult, float(REGION), ALU.add)
            tt(past, tile_no_sb[:].unsqueeze(2).to_broadcast([P, TILES, E]), over[:].unsqueeze(1).to_broadcast([P, TILES, E]), ALU.is_ge)
            tt(skips, past, steps_of[:].unsqueeze(1).to_broadcast([P, TILES, E]), ALU.mult)
            add_up(first, past)
            ts(tab[:, 0:TILES], first, float(E - 1), ALU.min)
            add_up(rows, skips)
            nc.vector.scalar_tensor_tensor(out=tab[:, 72:72 + TILES], in0=tile_no_sb[:], scalar=float(TR), in1=rows,
                                           op0=ALU.mult, op1=ALU.add).then_inc(tab_ready, 1)

            NS = NBLK * BT * K
            where = slots_all[:].rearrange("p b n -> p (b n)")
            starts = rank[:, 0, BT]
            after_start = flat[:, 0:NS * (E - 1)].rearrange("p (n e) -> p n e", e=E - 1)
            skipped = flat[:, NS * (E - 1):NS * E]
            dve.wait_ge(slots_kept, NBLK)
            ts(starts, lanes_sb[:], -float(REGION), ALU.mult, float(E * REGION), ALU.add)
            tt(after_start, where.unsqueeze(2).to_broadcast([P, NS, E - 1]), starts[:, 1:E].unsqueeze(1).to_broadcast([P, NS, E - 1]), ALU.is_ge)
            tt(after_start, after_start, steps_of[:, 0:E - 1].unsqueeze(1).to_broadcast([P, NS, E - 1]), ALU.mult)
            add_up(skipped, after_start)
            nc.vector.tensor_tensor(out=y_slots[:].rearrange("p b n -> p (b n)"), in0=where, in1=skipped, op=ALU.subtract).then_inc(y_slots_ready, 1)

            nc.vector.tensor_tensor(out=scores[:, 0], in0=top_all[:, 1], in1=top_all[:, 0], op=ALU.subtract).then_inc(routed, 1)
            dve.wait_ge(e2_done, 1)
            ts(scores[:, 0], scores[:, 1], 1.0, ALU.add)
            link(nc.vector.reciprocal(scores[:, 0], scores[:, 0]))
            tt(scores[:, 1], scores[:, 1], scores[:, 0], ALU.mult)

            def qstack(b, a):
                dve.wait_ge(qhi_done, NH * b.n + a + 1)
                nc.vector.scalar_tensor_tensor(out=stack[:, b.k, a], in0=qb[:, :], scalar=bq_sb[:, a:a + 1], in1=part_hi[:, a],
                                               op0=ALU.add, op1=ALU.subtract).then_inc(qst_ready, 1)

            def query_low(b, j):
                low_part(j, qs_free, 2 + NP * b.n + j + 1, qlo_ready)

            def kv_of(b):
                dve.wait_ge(qe_free, NE + NP * b.n)
                nc.vector.tensor_copy(kv_now[:].rearrange("p n s c -> p (n s c)"),
                                      kv_all[:, bass.ds(b.batch, 1)].rearrange("p o n s c -> p (o n s c)")).then_inc(kv_now_ready, 1)

            o4 = [o[:, 0:2 * H * C].rearrange("p (t h c) -> p t h c", t=2, c=C) for o in ob]

            def denominators(b):
                dve.wait_ge(qe_free, NE + NP * (b.n + 1))
                for g in range(2):
                    last = nc.vector.tensor_scalar(out=den[:, g], in0=o4[g][:, :, :, HD], scalar1=DEN_EPS, scalar2=None, op0=ALU.add)
                last.then_inc(nrm_step, 1)

            def reciprocals(b):
                dve.wait_ge(nrm_step, 2 * b.n + 1)
                nc.vector.reciprocal(den[:], den[:]).then_inc(nrm_step, 1)

            def divide(b):
                dve.wait_ge(nrm_step, 2 * b.n + 2)
                dve.wait_ge(aT_done, ONE + b.n)
                for g in range(2):
                    last = nc.vector.tensor_tensor(out=attn[:, 2 * g:2 * g + 2].rearrange("p t (h c) -> p t h c", c=HD),
                                                   in0=o4[g][:, :, :, 0:HD], in1=den[:, g].unsqueeze(3).to_broadcast([P, 2, H, HD]), op=ALU.mult)
                last.then_inc(attn_ready, 1)

            def residual(b):
                dve.wait_ge(proj_done, b.n + 1)
                dve.wait_ge(out_done[b.k], ONE + 16 * b.batch)
                dve.wait_ge(moe_ready, b.n + 1)
                nc.vector.tensor_tensor(out=res[:, b.k], in0=qb[:, :], in1=moe[:].rearrange("p t d -> p (t d)"),
                                        op=ALU.add).then_inc(res_ready, 1)

            def experts(b, r):
                if r == 0:
                    dve.wait_ge(gathered[b.k], 16 * K * BT * (b.batch + 1))
                    if not (type(b.n) is int and b.n == 0):
                        dve.wait_ge(res_ready, ONE + b.n)
                else:
                    dve.wait_ge(moe_half, b.n + 1)
                for t in range(BT):
                    prev = acc[:, bass.ds(b.n, 1), t * D:(t + 1) * D].rearrange("p o n -> p (o n)") if r == 0 else moe[:, t]
                    last = nc.vector.scalar_tensor_tensor(out=moe[:, t], in0=y_got[:, b.k, r * BT + t], scalar=scores[:, r, bass.ds(BT * b.n + t, 1)],
                                                          in1=prev, op0=ALU.mult, op1=ALU.add)
                last.then_inc(moe_ready if r else moe_half, 1)

            qown = (qmx_step, qmxh_step)

            def qbody(b):
                nb, nnb = after(b), after(b, 2)
                before = step_of(b, 0, UN, UN)
                before = before[0] if before else None
                for s in range(NP):
                    if nb and s == Q1_STEP:
                        qstack(nb, 1)
                    if nb:
                        maximum(tm[s % 2], qf_done, nb, s, qown)
                    if nb and s >= 1:
                        max_low(nb, s - 1, qown, qmx_ready)
                    elif s == 0 and before:
                        max_low(b, UN - 1, qown, qmx_ready)
                    if at := step_of(b, s, QLOW_LAG, NP):
                        query_low(*at)
                    if nb:
                        max_high(nb, s, qown)
                    if before and s == OUT_LAG:
                        denominators(before)
                        reciprocals(before)
                        divide(before)
                    if s == OUT_LAG and b.k == 0 and before:
                        kv_of(b)
                    if before and s == PROJ_STEP - 4:
                        experts(before, 0)
                    if before and s == PROJ_STEP - 3:
                        experts(before, 1)
                    if before and s == PROJ_STEP:
                        residual(before)
                    if nnb and s == Q0_STEP:
                        qstack(nnb, 0)

            z = Block(0, 0, 0)
            dve.wait_ge(kv_split, ONE + 2 * NB)
            nc.vector.tensor_copy(kv_now[:].rearrange("p n s c -> p (n s c)"),
                                  kv_all[:, 0].rearrange("p n s c -> p (n s c)")).then_inc(kv_now_ready, 1)
            qstack(z, 0)
            qstack(z, 1)
            for u in range(UN):
                maximum(tm[u % 2], qf_done, z, u, qown)
                max_high(z, u, qown)
                max_low(z, u, qown, qmx_ready)
            qstack(after(z), 0)

            dve.wait_ge(whi_done, 1)
            nc.vector.scalar_tensor_tensor(out=w1_lo[:], in0=w1_sb[:], scalar=W_SCALE, in1=w1_hi[:], op0=ALU.mult,
                                           op1=ALU.subtract).then_inc(w_ready, 1)
            dve.wait_ge(w_ready, 2)

            def tile_low(j):
                dve.wait_ge(thi_done, j.n + 1)
                nc.vector.tensor_tensor(out=xt_lo[:, j.i % 2], in0=xt_ps[j.i % 2][:, 0:TR], in1=xt_hi[:, j.i % 2],
                                        op=ALU.subtract).then_inc(tlo_done, 1)

            def hidden_second(j):
                e = expert_of(dve, j)
                dve.wait_ge(z_done[1], j.n + 1)
                if type(j.n) is not int or j.n >= 2:
                    dve.wait_ge(y_done, j.n - 1)
                nc.vector.tensor_scalar(out=hid[1][:, j.i % 2], in0=z_ps[1][j.i % 2][:, 0:TR], scalar1=b1_sb[:, bass.ds(HC * e + 1, 1)],
                                        scalar2=0.0, op0=ALU.add, op1=ALU.max).then_inc(h_ready[1], 1)

            def keep_y(j):
                e = expert_of(dve, j)
                dve.wait_ge(y_done, j.n + 1)
                if type(j.n) is not int or j.n >= NX:
                    dve.wait_ge(y_stored[j.i], 16 * j.g)
                nc.vector.tensor_tensor(out=y_tile[:, j.i], in0=y_ps[j.i % 2][:, 0:TR].rearrange("p (t d) -> p t d", d=D),
                                        in1=b2_sb[:, bass.ds(e, 1)].to_broadcast([P, TT, D]), op=ALU.add).then_inc(y_kept, 1)

            def tile_body(j):
                if later(j, 2):
                    tile_low(later(j, 2))
                if later(j, 1):
                    hidden_second(later(j, 1))
                keep_y(j)

            tile_low(tile(0))
            tile_low(tile(1))
            hidden_second(tile(0))
            over_tiles(dve, tile_body, 2)

            over_blocks(dve, qbody, 2)
            end = Block(NBLK - 1, PER - 1, NB - 1)
            query_low(end, NP - 1)
            denominators(end)
            reciprocals(end)
            divide(end)
            experts(end, 0)
            experts(end, 1)
            residual(end)

        @block.tensor
        def _(pe):
            nc.tensor.sem_inc(e_free, NE)
            pe.wait_ge(s_const, 2)
            pe.wait_ge(w_in, WAITS_W)
            mm = nc.tensor.matmul

            def turn_x(b):
                pe.wait_ge(xn_ready, b.n + 1)
                if not (type(b.n) is int and b.n == 0):
                    pe.wait_ge(kst_ready, NH * b.n)
                for t in range(BT):
                    last = nc.tensor.transpose(xk[:, t * P:(t + 1) * P], xn[:, b.k, t], ident_sb[:])
                last.then_inc(xT_done, 1)

            def keys(b, a):
                if a == 0:
                    pe.wait_ge(xT_kept, b.n + 1)
                else:
                    pe.wait_ge(kst_ready, NH * b.n + a)
                mm(xk[:, :], wk_sb[:, a], xnT[:, b.k], start=True, stop=True).then_inc(kT_done, 1)

            def values(b, j):
                if j:
                    pe.wait_ge(v_taken, 2 * b.n + j)
                elif not (type(b.n) is int and b.n == 0):
                    pe.wait_ge(rank_ready, b.n)
                w = D + E
                for t in range(2):
                    last = mm(vb[:, t * w:(t + 1) * w], xnT[:, b.k, (2 * j + t) * P:(2 * j + t + 1) * P], wvg_sb[:],
                              start=(t == 0), stop=(t == 1), skip_group_check=True)
                last.then_inc(v_done, 1)

            def key_features(b, u):
                a, t = divmod(u, BT)
                if t == 0:
                    pe.wait_ge(kst_ready, NH * b.n + a + 1)
                pe.wait_ge(dp_free, UN * b.n + u + 1)
                w = stack[:, b.k, a, t * P:(t + 1) * P]
                mm(dp[u % 4][:, :], w, feat_hi[:], start=True, stop=False, skip_group_check=True)
                mm(dp[u % 4][:, :], w, feat_lo[:], start=False, stop=False, skip_group_check=True).then_inc(feat_done, 1)

            def turn_max(b, u):
                pe.wait_ge(mx_ready, UN * b.n + u + 1)
                pe.wait_ge(mxT_ready, ONE + UN * b.n + u)
                nc.tensor.transpose(mt16, mx16[:, u % NM], ident16[:]).then_inc(mxT_done, 1)

            def shift(b, u):
                pe.wait_ge(mxT_ready, ONE + UN * b.n + u + 1)
                mm(dp[u % 4][:, :], mxT[:, u % 2], sel_sb[:], start=False, stop=True, skip_group_check=True).then_inc(shifted, 1)

            def kv(b, u):
                a, t = divmod(u, BT)
                pe.wait_ge(elo_ready, UN * b.n + u + 1)
                if a == 0:
                    pe.wait_ge(vlo_done, 2 * b.n + t // 2 + 1)
                if b.k == 0 and u == 0:
                    pe.wait_ge(kv_taken, ONE + b.batch)
                for n in range(PH):
                    pr = a * PH + n
                    mm(kv_ps[:, pr].rearrange("p s c -> p (s c)"), e_hi[:, u % NE, n * P:(n + 1) * P],
                       v16[:, b.k, t, pr].rearrange("p s c -> p (s c)"), start=(b.k == 0 and u == 0 and n == 0),
                       stop=False, skip_group_check=True)
                    last = mm(kv_ps[:, pr, 0], e_lo[:, u % NE, n * P:(n + 1) * P], v16[:, b.k, t, pr, 0],
                              start=False, stop=(b.k == PER - 1 and u == UN - 1 and n == PH - 1), skip_group_check=True)
                last.then_inc(e_free, 1)

            def rank_in_block(b):
                pe.wait_ge(chosen_ready, b.n + 1)
                if not (type(b.n) is int and b.n == 0):
                    pe.wait_ge(rank_ready, b.n)
                c = chosen[:].rearrange("p t e -> p (t e)")
                mm(rank_ps, below_sb[:], c, start=True, stop=False, skip_group_check=True)
                for t in range(1, BT + 1):
                    last = mm(rank_ps[:, t * E:], ones_sb[:], c[:, 0:(BT + 1 - t) * E], start=False, stop=(t == BT), skip_group_check=True)
                last.then_inc(rank_done, 1)

            def body(b):
                nb = after(b)
                for s in range(UN):
                    if at := step_of(b, s, TURN_LAG, UN):
                        turn_max(*at)
                    key_features(b, s)
                    if s == RANK_STEP:
                        rank_in_block(b)
                    if at := step_of(b, s, KV_LAG, UN):
                        kv(*at)
                    if at := step_of(b, s, TURN_LAG, UN):
                        shift(*at)
                    if nb and s == XT_STEP:
                        turn_x(nb)
                    if nb and s == KT_STEP:
                        keys(nb, 0)
                    if nb and s == KT_STEP + 1:
                        keys(nb, 1)
                        values(nb, 0)
                    if nb and s == UN - 1:
                        values(nb, 1)

            z = Block(0, 0, 0)
            turn_x(z)
            keys(z, 0)
            keys(z, 1)
            values(z, 0)
            values(z, 1)
            over_blocks(pe, body, 1)
            end = Block(NBLK - 1, PER - 1, NB - 1)
            for u in range(UN - TURN_LAG, UN):
                turn_max(end, u)
                shift(end, u)
            for u in range(UN - KV_LAG, UN):
                kv(end, u)

            nc.tensor.sem_inc(qe_free, NE)
            pe.wait_ge(dp_free, 4 + UN * NBLK)
            pe.wait_ge(kv_split, ONE + 2 * NB)

            def queries(b, a):
                if a == 1:
                    pe.wait_ge(qst_ready, NH * b.n + 1)
                elif not (type(b.n) is int and b.n < 2):
                    pe.wait_ge(res_ready, ONE + b.n - 2)
                mm(qb[:, :], wq_sb[:, a], xnT_all[:, bass.ds(b.n, 1)].rearrange("p o n -> p (o n)"), start=True, stop=True).then_inc(qT_done, 1)

            def qfeat(b, u):
                a, t = divmod(u, BT)
                if t == 0:
                    pe.wait_ge(qst_ready, NH * b.n + a + 1)
                if not (type(b.n) is int and b.n == 0 and u < 2):
                    pe.wait_ge(qmx_step, UN * b.n + u - 1)
                w = stack[:, b.k, a, t * P:(t + 1) * P]
                mm(tm[u % 2][:, :], w, feat_hi[:], start=True, stop=False)
                mm(tm[u % 2][:, :], w, feat_lo[:], start=False, stop=True).then_inc(qf_done, 1)

            def qturn(b, u):
                pe.wait_ge(qmx_ready, UN * b.n + u + 1)
                if u or not (type(b.n) is int and b.n == 0):
                    pe.wait_ge(qmxT_ready, UN * b.n + u)
                nc.tensor.transpose(mt16, mx16[:, u % NM], ident16[:]).then_inc(qmxT_done, 1)

            def qshifted(b, j):
                a, n = divmod(j, PH)
                if n == 0:
                    pe.wait_ge(qmxT_ready, UN * b.n + (a + 1) * BT)
                pe.wait_ge(qs_free, NP * b.n + j + 1)
                f = slice(n * P, (n + 1) * P)
                mm(fm[j % 2][:, :], feat_hi[:, f], stack[:, b.k, a], start=True, stop=False)
                mm(fm[j % 2][:, :], feat_lo[:, f], stack[:, b.k, a], start=False, stop=False)
                mm(fm[j % 2][:, :], sel_sb[:, f], mxT_q[:, b.k, a], start=False, stop=True).then_inc(qs_done, 1)

            def weigh(b, j):
                pe.wait_ge(qlo_ready, NP * b.n + j + 1)
                if j == 0:
                    pe.wait_ge(attn_ready, ONE + b.n)
                    if b.k == 0:
                        pe.wait_ge(kv_now_ready, b.batch + 1)
                for t in range(BT):
                    o = ob[t // 2][:, (t % 2) * H * C + j * 2 * C:(t % 2) * H * C + (j + 1) * 2 * C]
                    c = slice(t * P, (t + 1) * P)
                    mm(o, e_hi[:, j % NE, c], kv_now[:, j, 0], start=(j == 0 and t % 2 == 0), stop=False, skip_group_check=True)
                    mm(o, e_hi[:, j % NE, c], kv_now[:, j, 1], start=False, stop=False, skip_group_check=True)
                    last = mm(o, e_lo[:, j % NE, c], kv_now[:, j, 0], start=False, stop=(j == NP - 1 and t % 2 == 1), skip_group_check=True)
                last.then_inc(qe_free, 1)

            def turn_attn(b):
                pe.wait_ge(attn_ready, ONE + b.n + 1)
                if after(b, 2):
                    pe.wait_ge(qst_ready, NH * (b.n + 2) + 2)
                else:
                    pe.wait_ge(res_ready, ONE + b.n)
                for t in range(BT):
                    last = nc.tensor.transpose(qb[:, t * P:(t + 1) * P], attn[:, t], ident_sb[:])
                last.then_inc(aT_done, 1)

            def project(b):
                pe.wait_ge(aT_ready, b.n + 1)
                for t in range(BT):
                    last = mm(qb[:, t * P:(t + 1) * P], attnT[:, t * P:(t + 1) * P], wp_sb[:], start=(t == 0), stop=(t == BT - 1), skip_group_check=True)
                last.then_inc(proj_done, 1)

            def qbody(b):
                nb, nnb = after(b), after(b, 2)
                before = step_of(b, 0, UN, UN)
                before = before[0] if before else None
                for s in range(NP):
                    if nb and s == Q1_STEP:
                        queries(nb, 1)
                    qshifted(b, s)
                    if nb:
                        qfeat(nb, s)
                    if at := turned(b, s):
                        qturn(*at)
                    if at := step_of(b, s, OUT_LAG, NP):
                        weigh(*at)
                    if before and s == AT_STEP:
                        turn_attn(before)
                    if before and s == PROJ_STEP:
                        project(before)
                    if nnb and s == Q0_STEP:
                        queries(nnb, 0)

            z = Block(0, 0, 0)
            queries(z, 0)
            queries(z, 1)
            for u in range(UN):
                qfeat(z, u)
                qturn(z, u)
            queries(after(z), 0)

            pe.wait_ge(w_ready, 2)
            pe.wait_ge(qst_ready, NH + 1)

            def turn_tile(j):
                pe.wait_ge(tile_in[j.i], 16 * j.g + 16)
                if type(j.n) is not int or j.n >= 2:
                    pe.wait_ge(tlo_done, j.n - 1)
                for t in range(TT):
                    last = nc.tensor.transpose(xt_ps[j.i % 2][:, t * P:(t + 1) * P], x_tile[:, j.i, t], ident_sb[:])
                last.then_inc(tile_turned, 1)

            def hidden(j):
                e = expert_of(pe, j)
                pe.wait_ge(tlo_done, j.n + 1)
                hi, lo = xt_hi[:, j.i % 2], xt_lo[:, j.i % 2]
                for c in range(HC):
                    o, w = z_ps[c][j.i % 2][:, 0:TR], [v[:, bass.ds(e, 1), c * P:(c + 1) * P] for v in (w1_hi, w1_lo)]
                    mm(o, w[0], hi, start=True, stop=False)
                    mm(o, w[0], lo, start=False, stop=False)
                    mm(o, w[1], hi, start=False, stop=True).then_inc(z_done[c], 1)

            def result(j):
                e = expert_of(pe, j)
                pe.wait_ge(h_ready[0], j.n + 1)
                pe.wait_ge(h_ready[1], j.n + 1)
                if type(j.n) is not int or j.n >= 2:
                    pe.wait_ge(y_kept, j.n - 1)
                for t in range(TT):
                    for c in range(HC):
                        last = mm(y_ps[j.i % 2][:, t * P:(t + 1) * P], hid[c][:, j.i % 2, t * P:(t + 1) * P],
                                  w2_sb[:, bass.ds(HC * e + c, 1)], start=(t == 0 and c == 0), stop=(t == TT - 1 and c == HC - 1),
                                  skip_group_check=True)
                last.then_inc(y_done, 1)

            def tile_body(j):
                if later(j, 2):
                    turn_tile(later(j, 2))
                if later(j, 1):
                    hidden(later(j, 1))
                result(j)

            turn_tile(tile(0))
            turn_tile(tile(1))
            hidden(tile(0))
            over_tiles(pe, tile_body, 2)
            pe.wait_ge(y_kept, TILES)

            over_blocks(pe, qbody, 2)
            end = Block(NBLK - 1, PER - 1, NB - 1)
            for j in range(NP - OUT_LAG, NP):
                weigh(end, j)
            turn_attn(end)
            project(end)


_SHAPES = dict(D=128, H=16, M=64, E=8, HF=256)


def kernel(L0_attn_x, L0_attn_qkv_w, L0_attn_qkv_b, L0_attn_proj_w, L0_attn_proj_b, L0_attn_projection_matrix,
           L0_ffn_Wg, L0_ffn_W1, L0_ffn_b1, L0_ffn_W2, L0_ffn_b2):
    import numpy as np
    import concourse.bacc as bacc
    from concourse.bass_utils import run_bass_kernel_spmd
    D, H, M, E, HF = (_SHAPES[k] for k in ("D", "H", "M", "E", "HF"))
    HD, HH = D // H, H // 2
    a = [np.asarray(v) for v in (L0_attn_x, L0_attn_qkv_w, L0_attn_qkv_b, L0_attn_proj_w, L0_attn_proj_b,
                                 L0_attn_projection_matrix, L0_ffn_Wg, L0_ffn_W1, L0_ffn_b1, L0_ffn_W2, L0_ffn_b2)]
    x, qkv_w, qkv_b, proj_w, proj_b, pm, wg, w1, b1, w2, b2 = a

    def twice(w):
        h = w.reshape(2, D // 2, -1)
        return np.concatenate([h, h], axis=1)

    feat = np.zeros((2, HH, HD, HH, M), pm.dtype)
    for h in range(HH):
        feat[:, h, :, h, :] = pm.T
    sel = np.zeros((128, HH, M), np.float16)
    for h in range(HH):
        sel[[h, HH + h], h, :] = 1
    low = np.zeros((128, 1), np.float32)
    low[64:] = 1
    arrays = {
        "x": x,
        "wk2": twice(qkv_w[D:2 * D]).transpose(2, 0, 1),
        "wq2": twice(qkv_w[0:D]).transpose(2, 0, 1),
        "wvg": np.concatenate([qkv_w[2 * D:].T, wg], axis=1),
        "bk2": twice(qkv_b[D:2 * D])[:, :, 0].T,
        "bq2": twice(qkv_b[0:D])[:, :, 0].T,
        "bv": np.broadcast_to(qkv_b[2 * D:], (128, D)),
        "wp": proj_w.T,
        "bp": np.broadcast_to(proj_b, (128, D)),
        "feat": feat.reshape(128, HH * M),
        "sel": sel.reshape(128, HH * M),
        "split": low,
        "ident": np.eye(128, dtype=np.float32),
        "w1": w1.transpose(1, 0, 2),
        "b1": b1.reshape(E * HF // 128, 128).T,
        "w2": w2.reshape(E * HF // 128, 128, D).transpose(1, 0, 2),
        "b2": np.broadcast_to(b2, (128, E, D)),
        "lanes": np.broadcast_to(np.arange(E, 0, -1, dtype=np.float32), (128, E)),
        "tile_no": np.broadcast_to(np.arange(x.shape[0] * x.shape[1] * 2 // 256 + E - 1, dtype=np.float32), (128, x.shape[0] * x.shape[1] * 2 // 256 + E - 1)),
        "below": np.triu(np.ones((128, 128), np.float16), 1),
        "ones": np.ones((128, 128), np.float16),
    }
    nc = bacc.Bacc("TRN2", target_bir_lowering=False, num_devices=1)
    ins, aps = {}, []
    for name, v in arrays.items():
        v = np.ascontiguousarray(v)
        ins[f"in_{name}"] = v
        aps.append(nc.dram_tensor(f"in_{name}", v.shape, mybir.dt.from_np(v.dtype), kind="ExternalInput").ap())
    out = nc.dram_tensor("out_0", x.shape, mybir.dt.from_np(x.dtype), kind="ExternalOutput").ap()
    favor_moe_block(nc, *aps, out)
    r = run_bass_kernel_spmd(nc, [ins], core_ids=[0])
    return r.results[0]["out_0"]
```

```python
import concourse.bass as bass
from concourse import mybir
from collections import namedtuple
from contextlib import ExitStack

F32 = mybir.dt.float32
F16 = mybir.dt.float16
I32 = mybir.dt.int32
U32 = mybir.dt.uint32
ALU = mybir.AluOpType
ACT = mybir.ActivationFunctionType
AX = mybir.AxisListType
TENSOR, VECTOR, ACTIVATION, SYNC = mybir.EngineType.PE, mybir.EngineType.DVE, mybir.EngineType.Activation, mybir.EngineType.SP


def favor_moe_block(nc, x, wk2, wq2, wvg, bk2, bq2, bv, wp, bp, feat, sel, split, ident, w1, b1, w2, b2, lanes, tile_no, below, ones, out):
    NB, S, D = x.shape
    P = 128
    BT = 4
    BW = BT * P
    NBLK = NB * S // BW
    PER = S // BW
    H, M = 16, 64
    HD = D // H
    NH = 2
    HH = H // NH
    FW = HH * M
    NP = H // 2
    PH = NP // NH
    UN = NH * BT
    C = HD + 1
    E, HF = w1.shape[1], w1.shape[2]
    HC = HF // P
    K = 2
    TR = 256
    TT = TR // P
    TILES = NB * S * K // TR + E - 1
    REGION = NB * S + TR
    SPARE = (E - 1) * TR
    ROWS = E * REGION + SPARE
    ROW_AT = -(-TILES // E) * E
    START_AT = 2 * ROW_AT
    W_SCALE = 2.0 ** 6
    EPS = 1e-6
    LIFT = 14
    LIFT_BIAS = LIFT * 0.6931471805599453
    FEAT_EPS = EPS * M ** 0.5 * 2.0 ** LIFT
    EPS_HI = round(FEAT_EPS * 2 ** 12) / 2 ** 12
    KV_SCALE = 2.0 ** -15
    DEN_EPS = EPS * M * 2.0 ** (2 * LIFT) * KV_SCALE

    xv = x.rearrange("b (k t p) d -> p (b k) t d", p=P, t=BT)
    ov = out.rearrange("b (k t p) d -> p (b k) t d", p=P, t=BT)

    with ExitStack() as ctx:
        def sb(name, shape, dt=F32):
            return ctx.enter_context(nc.sbuf_tensor(name, shape, dt))

        def sem(name):
            return ctx.enter_context(nc.semaphore(name))

        wk_sb, wq_sb = sb("wk_sb", [P, NH, P]), sb("wq_sb", [P, NH, P])
        wvg_sb = sb("wvg_sb", [P, D + E])
        bk_sb, bq_sb = sb("bk_sb", [P, NH]), sb("bq_sb", [P, NH])
        bv_sb, bp_sb = sb("bv_sb", [P, D]), sb("bp_sb", [P, D])
        wp_sb = sb("wp_sb", [P, D])
        feat_sb = sb("feat_sb", [P, FW])
        feat_hi, feat_lo = sb("feat_hi", [P, FW], F16), sb("feat_lo", [P, FW], F16)
        sel_sb = sb("sel_sb", [P, FW], F16)
        eps_hi, eps_lo = sb("eps_hi", [P, P], F16), sb("eps_lo", [P, P], F16)
        low_rows = sb("low_rows", [P, 1])
        bk_low, bq_low = sb("bk_low", [P, NH]), sb("bq_low", [P, NH])
        ident_sb = sb("ident_sb", [P, P])
        ident16 = sb("ident16", [P, P], F16)
        lift_sb, table_on = sb("lift_sb", [P, 1]), sb("table_on", [P, 1])
        half_pow = sb("half_pow", [P, BT])
        w1_sb = sb("w1_sb", [P, E, HF])
        w1_hi, w1_lo = sb("w1_hi", [P, E, HF], F16), sb("w1_lo", [P, E, HF], F16)
        b1_sb = sb("b1_sb", [P, HC * E])
        w2_sb = sb("w2_sb", [P, HC * E, D])
        b2_sb = sb("b2_sb", [P, E, D])
        lanes_sb = sb("lanes_sb", [P, E])
        tile_no_sb = sb("tile_no_sb", [P, TILES])
        below_sb, ones_sb = sb("below_sb", [P, P], F16), sb("ones_sb", [P, P], F16)
        zeros = sb("zeros", [P, P])
        acc = sb("acc", [P, NBLK, BW])
        xnT_all = sb("xnT_all", [P, NBLK, BW])
        top_all = sb("top_all", [P, K, NBLK * BT])
        scores = sb("scores", [P, K, NBLK * BT])
        slots_all = sb("slots_all", [P, NBLK, K * BT])
        y_slots = sb("y_slots", [P, NBLK, K * BT], U32)
        kv_all = sb("kv_all", [P, NB, NP, 2, 2 * C], F16)
        xb = sb("xb", [P, PER, BT, D])
        xn = sb("xn", [P, PER, BT, D])
        stat, mv = sb("stat", [P, BT, 6]), sb("mv", [P, BT, 2])
        veps, rstd = sb("veps", [P, BT]), sb("rstd", [P, BT])
        xnT = sb("xnT", [P, PER, BW])
        part_hi = sb("part_hi", [P, NH, BW], F16)
        stack = sb("stack", [P, PER, NH, BW], F16)
        v32 = sb("v32", [P, 2, 2 * P])
        v16 = sb("v16", [P, PER, BT, NP, 2, 2 * C], F16)
        NE = 8
        e_hi = sb("e_hi", [P, NE, FW], F16)
        e_32 = sb("e_32", [P, NE, FW])
        e_lo = sb("e_lo", [P, NE, FW], F16)
        NM = 4
        mx = sb("mx", [P, NM, HH])
        mx16 = sb("mx16", [P, NM, P], F16)
        mxT = sb("mxT", [P, 2, P], F16)
        mxT_q = sb("mxT_q", [P, PER, NH, BW], F16)
        kv_low, kv32 = sb("kv_low", [P, NP, 2 * C]), sb("kv32", [P, NP, 2 * C])
        kv_now = sb("kv_now", [P, NP, 2, 2 * C], F16)
        den = sb("den", [P, 2, 2, H])
        attn = sb("attn", [P, BT, D])
        attnT = sb("attnT", [P, BW])
        res = sb("res", [P, PER, BW])
        logits = sb("logits", [P, PER, BT, E])
        logits_left = sb("logits_left", [P, BT, E])
        marked, lane_key = sb("marked", [P, BT, E]), sb("lane_key", [P, BT])
        row_if_chosen = sb("row_if_chosen", [P, K, BT, E])
        is_choice = sb("is_choice", [P, K, BT, E])
        chosen = sb("chosen", [P, BT + 1, E], F16)
        rank = sb("rank", [P, PER, BT + 1, E])
        slot32, slot = sb("slot32", [P, K * BT]), sb("slot", [P, PER, K * BT], U32)
        cnt, steps_of, over = sb("cnt", [P, E]), sb("steps_of", [P, E]), sb("over", [P, E])
        tab = sb("tab", [P, START_AT + E], I32)
        NX = 4
        x_tile = sb("x_tile", [P, NX, TT, D])
        xt_hi, xt_lo = sb("xt_hi", [P, 2, TR], F16), sb("xt_lo", [P, 2, TR], F16)
        hid = [sb("hid0", [P, 2, TR]), sb("hid1", [P, 2, TR])]
        y_tile = sb("y_tile", [P, NX, TT, D])
        y_got = sb("y_got", [P, PER, K * BT, D])
        score_now = sb("score_now", [P, PER, K, BT])
        moe = xb[:, 0]
        x_rows = nc.dram_tensor("x_rows", [ROWS, D], F32, kind="Internal").ap()
        y_rows = nc.dram_tensor("y_rows", [TILES * TR, D], F32, kind="Internal").ap()
        bank = [ctx.enter_context(nc.psum_tensor(f"bank{n}", [P, 512], F32)) for n in range(8)]

        block = ctx.enter_context(nc.Block())
        def sems(names):
            return [sem(n) for n in names.split()]

        w_sp, w_act, w_late, s_const, pow_const = sems("w_sp w_act w_late s_const pow_const")
        x_in = [sem(f"x_in{k}") for k in range(PER)]
        stats_done, rstd_done, xn_ready, acc_ready = sems("stats_done rstd_done xn_ready acc_ready")
        xT_done, xT_kept, kT_done, khi_done, kst_ready = sems("xT_done xT_kept kT_done khi_done kst_ready")
        v_done, v_taken, vhi_done, vlo_done = sems("v_done v_taken vhi_done vlo_done")
        feat_done, mx_ready, mxT_done, mxT_ready, shifted = sems("feat_done mx_ready mxT_done mxT_ready shifted")
        dp_free, elo_ready, e_free = sem("dp_free"), sems("elo_ready elo_pool"), sem("e_free")
        kvlow_done, kv_taken, kvhi_done, kv_split = sems("kvlow_done kv_taken kvhi_done kv_split")
        dve_step, ln_step, mx_step, mxh_step = sems("dve_step ln_step mx_step mxh_step")
        qmx_step, qmxh_step, nrm_step, choice_step = sems("qmx_step qmxh_step nrm_step choice_step")
        routed, e2_done, e2_used = sems("routed e2_done e2_used")
        chosen_ready, rank_done, rank_ready = sems("chosen_ready rank_done rank_ready")
        slot_part, slot_ready, slots_kept, y_slots_ready = sems("slot_part slot_ready slots_kept y_slots_ready")
        scattered = [sem(f"scattered{k}") for k in range(PER)]
        tab_ready, zeroed, zeroed_act = sems("tab_ready zeroed zeroed_act")
        whi_done, w_ready = sems("whi_done w_ready")
        tile_in, y_stored = [sem(f"tile_in{n}") for n in range(NX)], [sem(f"y_stored{n}") for n in range(NX)]
        tile_turned, thi_done, tlo_done = sems("tile_turned thi_done tlo_done")
        z_done, h_ready = sems("z0_done z1_done"), sems("h0_ready h1_ready")
        y_done, y_kept = sems("y_done y_kept")
        slot_step, score_ready, moe_half, moe_ready = sems("slot_step score_ready moe_half moe_ready")
        gathered = [sem(f"gathered{k}") for k in range(PER)]
        qT_done, qhi_done, qst_ready = sems("qT_done qhi_done qst_ready")
        qf_done, qmx_ready, qmxT_done, qmxT_ready = sems("qf_done qmx_ready qmxT_done qmxT_ready")
        qs_done, qlo_ready, qe_free, qs_free = sem("qs_done"), sems("qlo_ready qlo_pool"), sem("qe_free"), sem("qs_free")
        kv_now_ready, attn_ready, aT_done, aT_ready = sems("kv_now_ready attn_ready aT_done aT_ready")
        proj_done, res_ready = sems("proj_done res_ready")
        out_done = [sem(f"out_done{k}") for k in range(PER)]

        dp = bank[0:4]
        xk, vb, mt, kvb = bank[4], bank[5], bank[6], bank[7]
        mt16 = mt[:, 0:64].bitcast(F16)
        kv_ps = kvb[:, 0:NP * 4 * C].rearrange("p (n s c) -> p n s c", n=NP, s=2)
        tm, fm, ob = bank[0:2], bank[2:4], bank[4:6]
        qb = bank[7]
        rank_ps = vb[:, 2 * (D + E):2 * (D + E) + (BT + 1) * E]
        xt_ps, z_ps, y_ps = bank[0:2], [bank[2:4], bank[6:8]], bank[4:6]

        def turned(b, s):
            if s >= QTURN_LAG:
                return (after(b), s - QTURN_LAG) if after(b) else None
            return None if type(b.n) is int and b.n == 0 else (b, s - QTURN_LAG + UN)

        TURN_LAG, EXP_LAG, LOW_LAG, KV_LAG = 2, 3, 5, 7
        XT_STEP, KT_STEP = 3, 5
        RANK_STEP = 3
        QTURN_LAG, QLOW_LAG = 2, 1
        Q1_STEP, Q0_STEP = 0, 4
        DIV_STEP, AT_STEP, PROJ_STEP, WEIGH_STEP = 2, 4, 5, 6

        early_sp = [(ident_sb[:], ident), (feat_sb[:], feat), (bk_sb[:], bk2), (low_rows[:], split), (lanes_sb[:], lanes),
                    (bq_sb[:], bq2)]
        early_act = [(wk_sb[:], wk2), (wvg_sb[:], wvg), (bv_sb[:], bv), (sel_sb[:], sel), (bp_sb[:], bp), (below_sb[:], below),
                     (ones_sb[:], ones)]
        late = [(tile_no_sb[:], tile_no), (wq_sb[:], wq2), (wp_sb[:], wp), (w1_sb[:], w1), (b1_sb[:], b1), (w2_sb[:], w2),
                (b2_sb[:], b2)]

        KEYS_POOL, QUERIES_POOL = (3, 5, 7), (2,)

        def low_count(on_pool, n, u):
            mine = [v for v in range(UN) if (v in on_pool) == (u in on_pool)]
            return u in on_pool, len(mine) * n + mine.index(u) + 1

        Block = namedtuple("Block", "n k batch")

        def after(b, ahead=1):
            for _ in range(ahead):
                b = Block(b.n + 1, (b.k + 1) % PER, b.batch + 1 if b.k == PER - 1 else b.batch)
            return None if type(b.n) is int and b.n >= NBLK else b

        def over_blocks(eng, body, ahead):
            body(Block(0, 0, 0))
            pairs = (NBLK - 1 - ahead) // PER
            with eng.Fori(0, pairs) as i:
                body(Block(PER * i + 1, 1, i))
                body(Block(PER * i + 2, 0, i + 1))
            for n in range(PER * pairs + 1, NBLK):
                body(Block(n, n % PER, n // PER))

        def step_of(b, s, lag, units):
            u = s - lag
            if u >= 0:
                return b, u
            if type(b.n) is int and b.n == 0:
                return None
            return Block(b.n - 1, (b.k + 1) % PER, b.batch if b.k else b.batch - 1), u + units

        ONE = 1
        from_one = [kv_taken, mxT_ready, kv_split, attn_ready, aT_done, res_ready] + out_done

        Tile = namedtuple("Tile", "n g i")

        def tile(n):
            return Tile(n, n // NX, n % NX)

        def later(j, by):
            if type(j.n) is int:
                return tile(j.n + by) if j.n + by < TILES else None
            return Tile(j.n + by, j.g + (j.i + by) // NX, (j.i + by) % NX)

        def experts_of(engine, n, count):
            return nc.values_load_multi_w_load_instructions(
                tab[0:1, bass.ds(n, count)], engines=(engine,), min_val=0, max_val=E - 1,
                skip_runtime_bounds_check_because="the table's experts are counts that a minimum keeps below E")[1]

        def over_tiles(eng, body, ahead, look_up):
            groups = (TILES - ahead) // NX

            def group(n, tiles):
                for j, found in zip(tiles, look_up(n, len(tiles))):
                    body(j, *found)

            group(0, [tile(n) for n in range(NX)])
            with eng.Fori(1, groups) as g:
                group(NX * g, [Tile(NX * g + i, g, i) for i in range(NX)])
            group(NX * groups, [tile(n) for n in range(NX * groups, TILES)])

        def experts_two(engine):
            def look_up(n, count):
                ex = experts_of(engine, n, min(count + 1, TILES - n) if type(n) is int else count + 1)
                return list(zip(ex, (*ex[1:], None)))
            return look_up

        def rows_of(engine, n, count):
            return nc.values_load_multi_w_load_instructions(
                tab[0:1, bass.ds(n + ROW_AT, count)], engines=(engine,), min_val=0, max_val=ROWS - TR,
                skip_runtime_bounds_check_because="a tile's rows end where its expert's region does, or the spare rows do")[1]

        def starts_of(engine, n, count):
            return nc.values_load_multi_w_load_instructions(
                tab[0:1, START_AT + n:START_AT + n + count], engines=(engine,), min_val=0, max_val=ROWS - TR,
                skip_runtime_bounds_check_because="an expert's region has room for every token and a tile of zeros")[1]

        def rows(ap, row):
            return ap[bass.ds(row, TR)].rearrange("(t p) d -> p t d", p=P)

        @block.sync
        def _(sp):
            for s in from_one:
                nc.sync.sem_inc(s, ONE)
            sp.dma_start(xb[:, 0], xv[:, 0]).then_inc(x_in[0], 16)
            for dst, src in early_sp:
                sp.dma_start(dst, src).then_inc(w_sp, 16)
            sp.dma_start(xb[:, 1], xv[:, 1]).then_inc(x_in[1], 16)
            for dst, src in late:
                sp.dma_start(dst, src).then_inc(w_late, 16)
            sp.wait_ge(s_const, 2)
            two = zeros[:].unsqueeze(1).to_broadcast([P, TT, D])
            for n in range(E - 1):
                sp.dma_start(rows(x_rows, E * REGION + n * TR), two).then_inc(zeroed, 16)
            with sp.Fori(1, NB) as i:
                for k in range(PER):
                    sp.wait_ge(xn_ready, PER * i + k - PER + 1)
                    sp.wait_ge(acc_ready, PER * i + k - PER + 1)
                    sp.dma_start(xb[:, k], xv[:, bass.ds(PER * i + k, 1)].rearrange("p o t d -> p (o t) d")).then_inc(x_in[k], 16)
            sp.wait_ge(tab_ready, 1)
            for start in starts_of(SYNC, 0, E // 2):
                sp.dma_start(rows(x_rows, start), two).then_inc(zeroed, 16)
            sp.wait_ge(zeroed, 16 * (E - 1 + E // 2))
            sp.wait_ge(zeroed_act, 16 * E // 2)
            for k in range(PER):
                sp.wait_ge(scattered[k], 16 * K * BT * NB)

            def load_tile(j, row):
                if type(j.n) is not int or j.n >= NX:
                    sp.wait_ge(tile_turned, j.n - NX + 1)
                sp.dma_start(x_tile[:, j.i], rows(x_rows, row)).then_inc(tile_in[j.i], 16)

            def rows_ahead(n, count):
                more = min(count, TILES - n - NX) if type(n) is int else count
                got = rows_of(SYNC, n + NX, more) if type(n) is not int or more > 0 else ()
                return [(got[i] if i < len(got) else None,) for i in range(count)]

            def tile_body(j, row_ahead):
                if later(j, NX):
                    load_tile(later(j, NX), row_ahead)
                sp.wait_ge(y_kept, j.n + 1)
                sp.dma_start(rows(y_rows, TR * j.n), y_tile[:, j.i]).then_inc(y_stored[j.i], 16)

            for n, row in enumerate(rows_of(SYNC, 0, NX)):
                load_tile(tile(n), row)
            over_tiles(sp, tile_body, NX, rows_ahead)
            with sp.Fori(0, NB) as i:
                for k in range(PER):
                    sp.wait_ge(res_ready, ONE + PER * i + k + 1)
                    sp.dma_start(ov[:, bass.ds(PER * i + k, 1)].rearrange("p o t d -> p (o t) d"),
                                 res[:, k].rearrange("p (t d) -> p t d", t=BT)).then_inc(out_done[k], 16)
            for k in range(PER):
                sp.wait_ge(out_done[k], ONE + 16 * NB)

        @block.gpsimd
        def _(pool):
            nc.gpsimd.memset(half_pow[:], -0.5).then_inc(pow_const, 1)
            pool.wait_ge(pow_const, 1)

            def rstds(b):
                pool.wait_ge(stats_done, b.n + 1)
                nc.gpsimd.tensor_tensor(out=rstd[:], in0=veps[:], in1=half_pow[:], op=ALU.pow).then_inc(rstd_done, 1)

            def residual(b):
                pool.wait_ge(x_in[b.k], 16 * b.batch + 16)
                nc.gpsimd.tensor_tensor(out=acc[:, bass.ds(b.n, 1)].rearrange("p o (t d) -> p (o t) d", d=D), in0=xb[:, b.k],
                                        in1=bp_sb[:].unsqueeze(1).to_broadcast([P, BT, D]), op=ALU.add).then_inc(acc_ready, 1)

            def values_low(b, j):
                pool.wait_ge(vhi_done, 2 * b.n + j + 1)
                d = v16[:, b.k, 2 * j:2 * j + 2].rearrange("p t n s (h c) -> p (t n) s h c", h=2)
                nc.gpsimd.tensor_tensor(out=d[:, :, 1, :, 0:HD], in0=v32[:, j].rearrange("p (n h c) -> p n h c", h=2, c=HD),
                                        in1=d[:, :, 0, :, 0:HD], op=ALU.subtract).then_inc(vlo_done, 1)

            def slots_kept_of(b):
                pool.wait_ge(slot_ready, b.n + 1)
                nc.gpsimd.tensor_copy(slots_all[:, bass.ds(b.n, 1)].rearrange("p o n -> p (o n)"), slot[:, b.k]).then_inc(slots_kept, 1)

            def dispatch(b, t):
                for r in range(K):
                    pool.indirect_dma_start(x_rows[:, :], bass.IndirectOffsetOnAxis(ap=slot[:, b.k, r * BT + t:r * BT + t + 1], axis=0),
                                            xn[:, b.k, t], None).then_inc(scattered[b.k], 16)

            def low_part(b, u, exps, count, ready):
                pool.wait_ge(exps, count)
                nc.gpsimd.tensor_tensor(out=e_lo[:, u % NE], in0=e_32[:, u % NE], in1=e_hi[:, u % NE], op=ALU.subtract).then_inc(ready, 1)

            def key_low(b, u):
                low_part(b, u, dp_free, 4 + UN * b.n + u + 1, elo_ready[1])

            def body(b):
                nb, before = after(b), step_of(b, 0, UN, UN)
                if before:
                    key_low(before[0], KEYS_POOL[1])
                if nb:
                    rstds(nb)
                if before:
                    key_low(before[0], KEYS_POOL[2])
                if nb:
                    residual(nb)
                slots_kept_of(b)
                dispatch(b, 0)
                dispatch(b, 1)
                key_low(b, KEYS_POOL[0])
                dispatch(b, 2)
                dispatch(b, 3)
                if nb:
                    for j in range(2):
                        values_low(nb, j)

            z = Block(0, 0, 0)
            rstds(z)
            pool.wait_ge(w_act, 16 * len(early_act))
            residual(z)
            for j in range(2):
                values_low(z, j)
            over_blocks(pool, body, 1)
            end = Block(NBLK - 1, PER - 1, NB - 1)
            key_low(end, KEYS_POOL[1])
            key_low(end, KEYS_POOL[2])

            for n in range(NX):
                pool.wait_ge(y_stored[n], 16 * len(range(n, TILES, NX)))

            def slots_of(b):
                nc.gpsimd.tensor_copy(slot[:, b.k], y_slots[:, bass.ds(b.n, 1)].rearrange("p o n -> p (o n)")).then_inc(slot_step, 1)

            def gather(b, part):
                if part == 0:
                    pool.wait_ge(slot_step, b.n + 1)
                    if not (type(b.n) is int and b.n < 2):
                        pool.wait_ge(moe_ready, b.n - 1)
                    if after(b):
                        if not (type(b.n) is int and b.n == 0):
                            pool.wait_ge(gathered[1 - b.k], 16 * K * BT * after(b).batch)
                        slots_of(after(b))
                for n in range(part * BT, (part + 1) * BT):
                    pool.indirect_dma_start(y_got[:, b.k, n], None, y_rows[:, :],
                                            bass.IndirectOffsetOnAxis(ap=slot[:, b.k, n:n + 1], axis=0)).then_inc(gathered[b.k], 16)

            def query_low(b, j):
                low_part(b, j, qs_free, 2 + NP * b.n + j + 1, qlo_ready[1])

            def experts(b):
                nc.gpsimd.tensor_copy(score_now[:, b.k], scores[:, :, bass.ds(BT * b.n, BT)]).then_inc(score_ready, 1)
                pool.wait_ge(score_ready, b.n + 1)
                pool.wait_ge(gathered[b.k], 16 * K * BT * (b.batch + 1))
                nc.gpsimd.tensor_tensor(out=y_got[:, b.k], in0=y_got[:, b.k],
                                        in1=score_now[:, b.k].rearrange("p r t -> p (r t)").unsqueeze(2).to_broadcast([P, K * BT, D]),
                                        op=ALU.mult).then_inc(moe_half, 1)
                if not (type(b.n) is int and b.n == 0):
                    pool.wait_ge(res_ready, ONE + b.n)
                pool.wait_ge(moe_half, 2 * b.n + 1)
                nc.gpsimd.tensor_tensor(out=moe[:], in0=y_got[:, b.k, 0:BT], in1=y_got[:, b.k, BT:K * BT], op=ALU.add).then_inc(moe_half, 1)
                pool.wait_ge(moe_half, 2 * b.n + 2)
                nc.gpsimd.tensor_tensor(out=moe[:], in0=moe[:], in1=acc[:, bass.ds(b.n, 1)].rearrange("p o (t d) -> p (o t) d", d=D),
                                        op=ALU.add).then_inc(moe_ready, 1)

            def qbody(b):
                nb = after(b)
                for part in range(2):
                    if part < len(QUERIES_POOL):
                        query_low(b, QUERIES_POOL[part])
                    if nb:
                        gather(nb, part)
                experts(b)

            pool.wait_ge(y_slots_ready, 1)
            slots_of(z)
            gather(z, 0)
            gather(z, 1)
            pool.wait_ge(e2_used, 1)
            over_blocks(pool, qbody, 2)

        @block.scalar
        def _(act):
            for dst, src in early_act:
                act.dma_start(dst, src).then_inc(w_act, 16)
            nc.scalar.sem_inc(dp_free, 4)
            act.wait_ge(s_const, 1)
            nc.scalar.activation(table_on[:], lift_sb[:], ACT.Exp)

            def keep_xT(b):
                act.wait_ge(xT_done, b.n + 1)
                nc.scalar.activation(xnT[:, b.k], xk[:, :], ACT.Copy)
                nc.scalar.activation(xnT_all[:, bass.ds(b.n, 1)].rearrange("p o n -> p (o n)"), xk[:, :], ACT.Copy).then_inc(xT_kept, 1)

            def keys_high(b, a):
                act.wait_ge(kT_done, NH * b.n + a + 1)
                nc.scalar.activation(part_hi[:, a], xk[:, :], ACT.Identity, scale=low_rows[:, 0:1],
                                     bias=bk_low[:, a:a + 1]).then_inc(khi_done, 1)

            def values_high(b, j):
                act.wait_ge(v_taken, 2 * b.n + j + 1)
                d = v16[:, b.k, 2 * j:2 * j + 2].rearrange("p t n s (h c) -> p (t n) s h c", h=2)
                nc.scalar.activation(d[:, :, 0, :, 0:HD], v32[:, j].rearrange("p (n h c) -> p n h c", h=2, c=HD),
                                     ACT.Copy).then_inc(vhi_done, 1)

            def keep_key_max(b, u):
                act.wait_ge(mxT_done, UN * b.n + u + 1)
                nc.scalar.activation(mxT[:, u % 2], mt16, ACT.Copy).then_inc(mxT_ready, 1)

            def key_exps(b, u):
                act.wait_ge(shifted, UN * b.n + u + 1)
                act.wait_ge(e_free, UN * b.n + u + 1)
                nc.scalar.activation(e_hi[:, u % NE], dp[u % 4][:, :], ACT.Exp, bias=lift_sb[:, 0:1])
                nc.scalar.activation(e_32[:, u % NE], dp[u % 4][:, :], ACT.Exp, bias=lift_sb[:, 0:1])\
                    .then_inc(dp_free, 1)

            def batch_high(batch):
                act.wait_ge(e_free, NE + UN * PER * (batch + 1))
                nc.scalar.activation(kv_low[:], kv_ps[:, :, 1, :], ACT.Copy, scale=KV_SCALE).then_inc(kvlow_done, 1)

            def batch_split(batch):
                act.wait_ge(kv_taken, ONE + batch + 1)
                kd = kv_all[:, bass.ds(batch, 1)].rearrange("p o n s c -> p (o n) s c")
                for g in range(2):
                    r, c = slice(64 * g, 64 * g + 64), slice(C * g, C * g + C)
                    nc.scalar.activation(kd[r, :, 0, c], kv32[r, :, c], ACT.Copy).then_inc(kvhi_done, 1)

            def experts_weights():
                act.wait_ge(w_late, 16 * len(late))
                nc.scalar.activation(w1_hi[:], w1_sb[:], ACT.Copy, scale=W_SCALE).then_inc(whi_done, 1)
                nc.scalar.activation(b1_sb[:], b1_sb[:], ACT.Copy, scale=W_SCALE)
                nc.scalar.activation(w2_sb[:], w2_sb[:], ACT.Copy, scale=1 / W_SCALE).then_inc(w_ready, 1)

            def body(b):
                nb = after(b)
                for s in range(UN):
                    if type(b.n) is int and b.n == NBLK - 1 and s == RANK_STEP + 3:
                        experts_weights()
                    if s == KV_LAG and (at := step_of(b, s, KV_LAG + 1, UN)) and b.k == 0:
                        batch_high(at[0].batch)
                    if at := step_of(b, s, TURN_LAG, UN):
                        keep_key_max(*at)
                    if at := step_of(b, s, EXP_LAG, UN):
                        key_exps(*at)
                    if s == KV_LAG and (at := step_of(b, s, KV_LAG + 1, UN)) and b.k == 0:
                        batch_split(at[0].batch)
                    if nb and s == XT_STEP + 1:
                        keep_xT(nb)
                    if nb and s == KT_STEP + 1:
                        keys_high(nb, 0)
                        values_high(nb, 0)
                    if nb and s == KT_STEP + 2:
                        values_high(nb, 1)
                    if s == 1 and step_of(b, s, UN, UN):
                        keys_high(b, 1)

            keep_xT(Block(0, 0, 0))
            act.wait_ge(s_const, 2)
            act.wait_ge(w_sp, 16 * len(early_sp))
            keys_high(Block(0, 0, 0), 0)
            values_high(Block(0, 0, 0), 0)
            keys_high(Block(0, 0, 0), 1)
            values_high(Block(0, 0, 0), 1)
            over_blocks(act, body, 1)
            end = Block(NBLK - 1, PER - 1, NB - 1)
            for s in range(EXP_LAG):
                if s < TURN_LAG:
                    keep_key_max(end, UN - TURN_LAG + s)
                key_exps(end, UN - EXP_LAG + s)
            batch_high(NB - 1)
            batch_split(NB - 1)

            act.wait_ge(tab_ready, 1)
            for start in starts_of(ACTIVATION, E // 2, E // 2):
                act.dma_start(rows(x_rows, start), zeros[:].unsqueeze(1).to_broadcast([P, TT, D])).then_inc(zeroed_act, 16)

            act.wait_ge(routed, 1)
            nc.scalar.activation(scores[:, 1], scores[:, 0], ACT.Exp).then_inc(e2_done, 1)

            nc.scalar.sem_inc(qs_free, 2)
            def queries_high(b, a):
                act.wait_ge(qT_done, NH * b.n + a + 1)
                nc.scalar.activation(part_hi[:, a], qb[:, :], ACT.Identity, scale=low_rows[:, 0:1],
                                     bias=bq_low[:, a:a + 1]).then_inc(qhi_done, 1)

            def keep_max(b, u):
                act.wait_ge(qmxT_done, UN * b.n + u + 1)
                a, t = divmod(u, BT)
                nc.scalar.activation(mxT_q[:, b.k, a, t * P:(t + 1) * P], mt16, ACT.Copy).then_inc(qmxT_ready, 1)

            def query_exps(b, j):
                act.wait_ge(qs_done, NP * b.n + j + 1)
                act.wait_ge(qe_free, NP * b.n + j + 1)
                nc.scalar.activation(e_hi[:, j % NE], fm[j % 2][:, :], ACT.Exp, bias=lift_sb[:, 0:1])
                nc.scalar.activation(e_32[:, j % NE], fm[j % 2][:, :], ACT.Exp, bias=lift_sb[:, 0:1])\
                    .then_inc(qs_free, 1)

            def keep_aT(b):
                act.wait_ge(aT_done, ONE + b.n + 1)
                nc.scalar.activation(attnT[:], ob[0][:, :], ACT.Copy).then_inc(aT_ready, 1)

            def qbody(b):
                nb, nnb = after(b), after(b, 2)
                for s in range(NP):
                    query_exps(b, s)
                    if at := turned(b, s):
                        keep_max(*at)
                    if nb and s == Q1_STEP + 1:
                        queries_high(nb, 1)
                    if s == AT_STEP and step_of(b, s, UN, UN):
                        keep_aT(step_of(b, s, UN, UN)[0])
                    if nnb and s == Q0_STEP + 1:
                        queries_high(nnb, 0)

            z = Block(0, 0, 0)
            queries_high(z, 0)
            queries_high(z, 1)
            for u in range(UN):
                keep_max(z, u)
            queries_high(after(z), 0)

            def tile_high(j):
                act.wait_ge(tile_turned, j.n + 1)
                if type(j.n) is not int or j.n >= 2:
                    act.wait_ge(z_done[1], j.n - 1)
                nc.scalar.activation(xt_hi[:, j.i % 2], xt_ps[j.i % 2][:, 0:TR], ACT.Copy).then_inc(thi_done, 1)

            def hidden_first(j, e):
                act.wait_ge(z_done[0], j.n + 1)
                if type(j.n) is not int or j.n >= 2:
                    act.wait_ge(y_done, j.n - 1)
                nc.scalar.activation(hid[0][:, j.i % 2], z_ps[0][j.i % 2][:, 0:TR], ACT.Relu,
                                     bias=b1_sb[:, bass.ds(HC * e, 1)]).then_inc(h_ready[0], 1)

            def tile_body(j, own, ahead):
                if later(j, 2):
                    tile_high(later(j, 2))
                if later(j, 1):
                    hidden_first(later(j, 1), ahead)

            act.wait_ge(w_ready, 2)
            tile_high(tile(0))
            tile_high(tile(1))
            hidden_first(tile(0), experts_of(ACTIVATION, 0, 1)[0])
            over_tiles(act, tile_body, 2, experts_two(ACTIVATION))

            over_blocks(act, qbody, 2)
            keep_aT(Block(NBLK - 1, PER - 1, NB - 1))

        @block.vector
        def _(dve):
            nc.vector.memset(lift_sb[:], LIFT_BIAS)
            nc.vector.memset(mx16[:], 0.0)
            nc.vector.memset(kv_all[:], 0.0)
            nc.vector.memset(zeros[:], 0.0)
            nc.vector.memset(chosen[:], 0.0)
            nc.vector.memset(eps_hi[:], EPS_HI)
            nc.vector.memset(eps_lo[:], FEAT_EPS - EPS_HI)
            nc.vector.memset(v16[:, :, :, :, 1], 0.0)
            nc.vector.memset(v16[:, :, :, :, 0], 1.0).then_inc(s_const, 1)
            SETUP = 2

            def stats(b):
                dve.wait_ge(x_in[b.k], 16 * b.batch + 16)
                if not (type(b.n) is int and b.n == 0):
                    dve.wait_ge(rstd_done, b.n)
                for t in range(BT):
                    last = nc.vector.bn_stats(out=stat[:, t], in_=xb[:, b.k, t])
                last.then_inc(ln_step, 1)

            def stats_seen(b):
                dve.wait_ge(ln_step, 2 * b.n + 1)

            def means(b):
                for t in range(BT):
                    last = nc.vector.bn_aggr(out=mv[:, t], in_=stat[:, t])
                last.then_inc(ln_step, 1)

            def variance(b):
                dve.wait_ge(ln_step, 2 * b.n + 2)
                nc.vector.tensor_scalar(out=veps[:], in0=mv[:, :, 1], scalar1=1e-5, scalar2=None, op0=ALU.add).then_inc(stats_done, 1)

            def normalise(b):
                dve.wait_ge(rstd_done, b.n + 1)
                if not (type(b.n) is int and b.n < 2):
                    dve.wait_ge(scattered[b.k], 16 * K * BT * b.batch)
                for t in range(BT):
                    last = nc.vector.tensor_scalar(out=xn[:, b.k, t], in0=xb[:, b.k, t], scalar1=mv[:, t, 0:1],
                                                   scalar2=rstd[:, t:t + 1], op0=ALU.subtract, op1=ALU.mult)
                last.then_inc(xn_ready, 1)

            def kstack(b, a):
                dve.wait_ge(khi_done, NH * b.n + a + 1)
                nc.vector.scalar_tensor_tensor(out=stack[:, b.k, a], in0=xk[:, :], scalar=bk_sb[:, a:a + 1], in1=part_hi[:, a],
                                               op0=ALU.add, op1=ALU.subtract).then_inc(kst_ready, 1)

            def values(b, j):
                dve.wait_ge(v_done, 2 * b.n + j + 1)
                if not (type(b.n) is int and b.n == 0):
                    dve.wait_ge(vlo_done, 2 * b.n + j - 1)
                vp = vb[:, 0:2 * (D + E)].rearrange("p (t c) -> p t c", t=2)
                nc.vector.tensor_tensor(out=v32[:, j].rearrange("p (t c) -> p t c", t=2), in0=vp[:, :, 0:D],
                                        in1=bv_sb[:].unsqueeze(1).to_broadcast([P, 2, D]), op=ALU.add)
                nc.vector.tensor_copy(logits[:, b.k, 2 * j:2 * j + 2], vp[:, :, D:D + E]).then_inc(v_taken, 1)

            def maximum(psum, done, b, u, own):
                dve.wait_ge(done, UN * b.n + u + 1)
                nc.vector.tensor_reduce(out=mx[:, u % NM], in_=psum[:, :].rearrange("p (h m) -> p h m", h=HH), axis=AX.X,
                                        op=ALU.max, negate=True).then_inc(own[0], 1)

            def max_high(b, u, own):
                dve.wait_ge(own[0], UN * b.n + u + 1)
                nc.vector.tensor_copy(mx16[:, u % NM, 0:HH], mx[:, u % NM]).then_inc(own[1], 1)

            def max_low(b, u, own, ready):
                dve.wait_ge(own[1], UN * b.n + u + 1)
                nc.vector.tensor_tensor(out=mx16[:, u % NM, HH:2 * HH], in0=mx[:, u % NM], in1=mx16[:, u % NM, 0:HH],
                                        op=ALU.subtract).then_inc(ready, 1)

            def low_part(u, exps, count, ready):
                dve.wait_ge(exps, count)
                nc.vector.scalar_tensor_tensor(out=e_lo[:, u % NE], in0=e_32[:, u % NE], scalar=FEAT_EPS, in1=e_hi[:, u % NE],
                                               op0=ALU.add, op1=ALU.subtract).then_inc(ready, 1)

            def key_low(b, u):
                if u not in KEYS_POOL:
                    low_part(u, dp_free, 4 + UN * b.n + u + 1, elo_ready[0])

            def batch_low(batch):
                dve.wait_ge(kv_split, ONE + 2 * batch)
                dve.wait_ge(kvlow_done, batch + 1)
                nc.vector.scalar_tensor_tensor(out=kv32[:], in0=kv_ps[:, :, 0, :], scalar=KV_SCALE, in1=kv_low[:],
                                               op0=ALU.mult, op1=ALU.add).then_inc(kv_taken, 1)

            def batch_split(batch):
                kd = kv_all[:, bass.ds(batch, 1)].rearrange("p o n s c -> p (o n) s c")
                dve.wait_ge(kvhi_done, 2 * batch + 2)
                for g in range(2):
                    r, c = slice(64 * g, 64 * g + 64), slice(C * g, C * g + C)
                    nc.vector.tensor_tensor(out=kd[r, :, 1, c], in0=kv32[r, :, c], in1=kd[r, :, 0, c],
                                            op=ALU.subtract).then_inc(kv_split, 1)

            bc = lambda v: v.unsqueeze(2).to_broadcast([P, BT, E])
            lanes_bc = lanes_sb[:].unsqueeze(1).to_broadcast([P, BT, E])
            CHOOSE = 12

            def choose(b, n):
                r, part = divmod(n, 6)
                if n == 0:
                    dve.wait_ge(v_taken, 2 * b.n + 2)
                else:
                    dve.wait_ge(choice_step, (CHOOSE - 1) * b.n + n)
                if n == 4 and not (type(b.n) is int and b.n == 0):
                    dve.wait_ge(slot_ready, b.n)
                src = logits_left[:] if r else logits[:, b.k]
                if part == 0:
                    op = nc.vector.tensor_reduce(out=top_all[:, r, bass.ds(BT * b.n, BT)], in_=src, axis=AX.X, op=ALU.max)
                elif part == 1:
                    op = nc.vector.tensor_tensor(out=marked[:], in0=src, in1=bc(top_all[:, r, bass.ds(BT * b.n, BT)]), op=ALU.is_equal)
                elif part == 2:
                    op = nc.vector.tensor_tensor(out=marked[:], in0=marked[:], in1=lanes_bc, op=ALU.mult)
                elif part == 3:
                    op = nc.vector.tensor_reduce(out=lane_key[:], in_=marked[:], axis=AX.X, op=ALU.max)
                elif part == 4:
                    op = nc.vector.tensor_tensor(out=is_choice[:, r], in0=lanes_bc, in1=bc(lane_key[:]), op=ALU.is_equal)
                elif r == 0:
                    op = nc.vector.scalar_tensor_tensor(out=logits_left[:], in0=is_choice[:, 0], scalar=-3e38, in1=src,
                                                        op0=ALU.mult, op1=ALU.add)
                else:
                    op = nc.vector.tensor_tensor(out=chosen[:, 0:BT], in0=is_choice[:, 0], in1=is_choice[:, 1], op=ALU.add)
                op.then_inc(chosen_ready if n == CHOOSE - 1 else choice_step, 1)

            def ranks(b):
                dve.wait_ge(rank_done, b.n + 1)
                nc.vector.tensor_tensor(out=rank[:, b.k], in0=rank_ps.rearrange("p (t e) -> p t e", e=E),
                                        in1=rank[:, 1 - b.k, BT].unsqueeze(1).to_broadcast([P, BT + 1, E]),
                                        op=ALU.add).then_inc(rank_ready, 1)

            def slots(b, part):
                if part == 0:
                    dve.wait_ge(rank_ready, b.n + 1)
                    nc.vector.tensor_tensor(out=row_if_chosen[:], in0=is_choice[:],
                                            in1=rank[:, b.k, 0:BT].unsqueeze(1).to_broadcast([P, K, BT, E]),
                                            op=ALU.mult).then_inc(slot_part, 1)
                elif part == 1:
                    dve.wait_ge(slot_part, 2 * b.n + 1)
                    nc.vector.tensor_reduce(out=slot32[:], in_=row_if_chosen[:].rearrange("p r t e -> p (r t) e"), axis=AX.X,
                                            op=ALU.add).then_inc(slot_part, 1)
                else:
                    dve.wait_ge(slot_part, 2 * b.n + 2)
                    nc.vector.tensor_copy(slot[:, b.k], slot32[:]).then_inc(slot_ready, 1)

            seen = [SETUP]

            def link(ins):
                seen[0] += 1
                ins.then_inc(dve_step, 1)
                dve.wait_ge(dve_step, seen[0])

            add_up = lambda out, in_: link(nc.vector.tensor_reduce(out=out, in_=in_, axis=AX.X, op=ALU.add))
            tt = lambda out, in0, in1, op: link(nc.vector.tensor_tensor(out=out, in0=in0, in1=in1, op=op))
            ts = lambda out, in0, a, op, b=None, op1=None: link(
                nc.vector.tensor_scalar(out=out, in0=in0, scalar1=a, scalar2=b, op0=op, **({"op1": op1} if op1 else {})))
            flat = y_got[:].rearrange("p k n d -> p (k n d)")
            most = NB * S // TR
            full = flat[:, 0:E * most].rearrange("p (e k) -> p e k", k=most)
            sums = flat[:, 0:E * E].rearrange("p (o e) -> p o e", e=E)
            past = flat[:, 0:TILES * E].rearrange("p (j e) -> p j e", e=E)
            skips = flat[:, TILES * E:2 * TILES * E].rearrange("p (j e) -> p j e", e=E)
            first = flat[:, 2 * TILES * E:2 * TILES * E + TILES]
            rows = flat[:, 2 * TILES * E + TILES:2 * TILES * E + 2 * TILES]
            ends = rank[:, (NBLK - 1) % PER, BT]

            def tables():
                dve.wait_ge(rank_ready, NBLK)
                nc.vector.tensor_copy(tab[:, START_AT:START_AT + E], ends)
                ts(cnt[:], lanes_sb[:], float(REGION), ALU.mult, -float(E * REGION), ALU.add)
                tt(cnt[:], cnt[:], ends, ALU.add)
                ts(cnt[:], cnt[:], 1.0 / TR, ALU.mult)
                tt(full, cnt[:].unsqueeze(2).to_broadcast([P, E, most]),
                   tile_no_sb[:, 0:most].unsqueeze(1).to_broadcast([P, E, most]), ALU.is_gt)
                add_up(steps_of[:], full)
                tt(sums, lanes_sb[:].unsqueeze(1).to_broadcast([P, E, E]), lanes_sb[:].unsqueeze(2).to_broadcast([P, E, E]), ALU.is_ge)
                tt(sums, sums, steps_of[:].unsqueeze(1).to_broadcast([P, E, E]), ALU.mult)
                add_up(over[:], sums)
                ts(steps_of[:], steps_of[:], -float(TR), ALU.mult, float(REGION), ALU.add)
                tt(past, tile_no_sb[:].unsqueeze(2).to_broadcast([P, TILES, E]),
                   over[:].unsqueeze(1).to_broadcast([P, TILES, E]), ALU.is_ge)
                tt(skips, past, steps_of[:].unsqueeze(1).to_broadcast([P, TILES, E]), ALU.mult)
                add_up(first, past)
                ts(tab[:, 0:TILES], first, float(E - 1), ALU.min)
                add_up(rows, skips)
                nc.vector.scalar_tensor_tensor(out=tab[:, ROW_AT:ROW_AT + TILES], in0=tile_no_sb[:], scalar=float(TR), in1=rows,
                                               op0=ALU.mult, op1=ALU.add).then_inc(tab_ready, 1)

            kown = (mx_step, mxh_step)

            def body(b):
                nb = after(b)
                for s in range(UN):
                    if at := step_of(b, s, 1, UN):
                        max_low(*at, kown, mx_ready)
                    if 4 * s < CHOOSE:
                        choose(b, 4 * s)
                    if s == RANK_STEP + 1:
                        slots(b, 0)
                    if at := step_of(b, s, LOW_LAG, UN):
                        key_low(*at)
                    if nb and s == 1:
                        stats_seen(nb)
                    if 4 * s < CHOOSE:
                        choose(b, 4 * s + 1)
                    if nb and s == KT_STEP + 1:
                        values(nb, 0)
                    if nb and s == KT_STEP + 2:
                        values(nb, 1)
                    if nb and s == 1:
                        means(nb)
                    if s == RANK_STEP + 1:
                        slots(b, 1)
                    if s == KV_LAG and (at := step_of(b, s, KV_LAG + 1, UN)) and b.k == 0:
                        batch_low(at[0].batch)
                    maximum(dp[s % 4], feat_done, b, s, kown)
                    if 4 * s < CHOOSE:
                        choose(b, 4 * s + 2)
                    if nb and s == 1:
                        variance(nb)
                    if type(b.n) is int and b.n == NBLK - 1 and s == RANK_STEP + 2:
                        tables()
                    if s == RANK_STEP + 1:
                        slots(b, 2)
                    max_high(b, s, kown)
                    if 4 * s < CHOOSE:
                        choose(b, 4 * s + 3)
                    if s == RANK_STEP:
                        ranks(b)
                    if nb and s == 0:
                        stats(nb)
                    if nb and s == XT_STEP - 1:
                        normalise(nb)
                    if nb and s == KT_STEP + 2:
                        kstack(nb, 0)
                    if s == 2 and step_of(b, 2, UN, UN):
                        kstack(b, 1)
                    if s == UN - 1 and (at := step_of(b, s, UN, UN)) and b.k == 0:
                        batch_split(at[0].batch)

            z = Block(0, 0, 0)
            stats(z)
            stats_seen(z)
            means(z)
            variance(z)
            normalise(z)
            dve.wait_ge(w_sp, 16 * len(early_sp))
            dve.wait_ge(w_act, 16 * len(early_act))
            nc.vector.tensor_copy(ident16[:], ident_sb[:])
            nc.vector.tensor_scalar(out=rank[:, PER - 1, BT], in0=lanes_sb[:], scalar1=-float(REGION), scalar2=float(E * REGION),
                                    op0=ALU.mult, op1=ALU.add)
            nc.vector.tensor_tensor(out=bk_low[:], in0=bk_sb[:], in1=low_rows[:].to_broadcast([P, NH]), op=ALU.mult)
            nc.vector.tensor_tensor(out=bq_low[:], in0=bq_sb[:], in1=low_rows[:].to_broadcast([P, NH]), op=ALU.mult)
            nc.vector.tensor_scalar(out=e_32[:, 0], in0=feat_sb[:], scalar1=float(HD) ** -0.5, scalar2=None,
                                    op0=ALU.mult).then_inc(dve_step, 1)
            dve.wait_ge(dve_step, 1)
            nc.vector.tensor_copy(feat_hi[:], e_32[:, 0]).then_inc(dve_step, 1)
            dve.wait_ge(dve_step, 2)
            nc.vector.tensor_tensor(out=feat_lo[:], in0=e_32[:, 0], in1=feat_hi[:], op=ALU.subtract).then_inc(s_const, 1)

            kstack(z, 0)
            values(z, 0)
            kstack(z, 1)
            values(z, 1)
            over_blocks(dve, body, 1)
            end = Block(NBLK - 1, PER - 1, NB - 1)
            max_low(end, UN - 1, kown, mx_ready)
            for u in range(UN - LOW_LAG, UN):
                key_low(end, u)
            batch_low(NB - 1)
            batch_split(NB - 1)

            nc.vector.tensor_tensor(out=scores[:, 0], in0=top_all[:, 1], in1=top_all[:, 0], op=ALU.subtract).then_inc(routed, 1)

            dve.wait_ge(whi_done, 1)
            nc.vector.scalar_tensor_tensor(out=w1_lo[:], in0=w1_sb[:], scalar=W_SCALE, in1=w1_hi[:], op0=ALU.mult,
                                           op1=ALU.subtract).then_inc(w_ready, 1)

            NS = NBLK * BT * K
            where = slots_all[:].rearrange("p b n -> p (b n)")
            starts = rank[:, 0, BT]
            after_start = flat[:, 0:NS * (E - 1)].rearrange("p (n e) -> p n e", e=E - 1)
            skipped = flat[:, NS * (E - 1):NS * E]

            def y_slots_part(part):
                if part == 0:
                    dve.wait_ge(slots_kept, NBLK)
                    ts(starts, lanes_sb[:], -float(REGION), ALU.mult, float(E * REGION), ALU.add)
                    tt(after_start, where.unsqueeze(2).to_broadcast([P, NS, E - 1]),
                       starts[:, 1:E].unsqueeze(1).to_broadcast([P, NS, E - 1]), ALU.is_ge)
                elif part == 1:
                    tt(after_start, after_start, steps_of[:, 0:E - 1].unsqueeze(1).to_broadcast([P, NS, E - 1]), ALU.mult)
                elif part == 2:
                    add_up(skipped, after_start)
                    nc.vector.tensor_tensor(out=y_slots[:].rearrange("p b n -> p (b n)"), in0=where, in1=skipped,
                                            op=ALU.subtract).then_inc(y_slots_ready, 1)
                else:
                    dve.wait_ge(e2_done, 1)
                    ts(scores[:, 0], scores[:, 1], 1.0, ALU.add)
                    link(nc.vector.reciprocal(scores[:, 0], scores[:, 0]))
                    nc.vector.tensor_tensor(out=scores[:, 1], in0=scores[:, 1], in1=scores[:, 0], op=ALU.mult).then_inc(e2_used, 1)

            def qstack(b, a):
                dve.wait_ge(qhi_done, NH * b.n + a + 1)
                nc.vector.scalar_tensor_tensor(out=stack[:, b.k, a], in0=qb[:, :], scalar=bq_sb[:, a:a + 1], in1=part_hi[:, a],
                                               op0=ALU.add, op1=ALU.subtract).then_inc(qst_ready, 1)

            def query_low(b, j):
                if j not in QUERIES_POOL:
                    low_part(j, qs_free, 2 + NP * b.n + j + 1, qlo_ready[0])

            def kv_of(b):
                dve.wait_ge(qe_free, NE + NP * b.n)
                nc.vector.tensor_copy(kv_now[:].rearrange("p n s c -> p (n s c)"),
                                      kv_all[:, bass.ds(b.batch, 1)].rearrange("p o n s c -> p (o n s c)")).then_inc(kv_now_ready, 1)

            o4 = [o[:, 0:2 * H * C].rearrange("p (t h c) -> p t h c", t=2, c=C) for o in ob]

            def denominators(b):
                dve.wait_ge(qe_free, NE + NP * (b.n + 1))
                for g in range(2):
                    last = nc.vector.tensor_scalar(out=den[:, g], in0=o4[g][:, :, :, HD], scalar1=DEN_EPS, scalar2=None, op0=ALU.add)
                last.then_inc(nrm_step, 1)

            def reciprocals(b):
                dve.wait_ge(nrm_step, 2 * b.n + 1)
                nc.vector.reciprocal(den[:], den[:]).then_inc(nrm_step, 1)

            def divide(b):
                dve.wait_ge(nrm_step, 2 * b.n + 2)
                dve.wait_ge(aT_done, ONE + b.n)
                for g in range(2):
                    last = nc.vector.tensor_tensor(out=attn[:, 2 * g:2 * g + 2].rearrange("p t (h c) -> p t h c", c=HD),
                                                   in0=o4[g][:, :, :, 0:HD], in1=den[:, g].unsqueeze(3).to_broadcast([P, 2, H, HD]),
                                                   op=ALU.mult)
                last.then_inc(attn_ready, 1)

            def residual(b):
                dve.wait_ge(proj_done, b.n + 1)
                dve.wait_ge(out_done[b.k], ONE + 16 * b.batch)
                dve.wait_ge(moe_ready, b.n + 1)
                nc.vector.tensor_tensor(out=res[:, b.k], in0=ob[1][:, :], in1=moe[:].rearrange("p t d -> p (t d)"),
                                        op=ALU.add).then_inc(res_ready, 1)

            qown = (qmx_step, qmxh_step)

            def qbody(b):
                nb, nnb = after(b), after(b, 2)
                before = step_of(b, 0, UN, UN)
                before = before[0] if before else None
                for s in range(NP):
                    if nb and s >= 1:
                        max_low(nb, s - 1, qown, qmx_ready)
                    elif s == 0 and before:
                        max_low(b, UN - 1, qown, qmx_ready)
                    if before and s == DIV_STEP:
                        denominators(before)
                    if before and s == PROJ_STEP + 1:
                        residual(before)
                    if nb and s == Q1_STEP + 2:
                        qstack(nb, 1)
                    if nnb and s == Q0_STEP + 2:
                        qstack(nnb, 0)
                    if at := step_of(b, s, QLOW_LAG, NP):
                        query_low(*at)
                    if before and s == DIV_STEP:
                        reciprocals(before)
                    if nb:
                        maximum(tm[s % 2], qf_done, nb, s, qown)
                    if before and s == DIV_STEP:
                        divide(before)
                    if nb:
                        max_high(nb, s, qown)
                    if s == DIV_STEP and b.k == 0 and before:
                        kv_of(b)

            z = Block(0, 0, 0)
            dve.wait_ge(kv_split, ONE + 2 * NB)
            nc.vector.tensor_copy(kv_now[:].rearrange("p n s c -> p (n s c)"),
                                  kv_all[:, 0].rearrange("p n s c -> p (n s c)")).then_inc(kv_now_ready, 1)
            qstack(z, 0)
            qstack(z, 1)
            for u in range(UN):
                maximum(tm[u % 2], qf_done, z, u, qown)
                max_high(z, u, qown)
                max_low(z, u, qown, qmx_ready)
            qstack(after(z), 0)

            dve.wait_ge(w_ready, 2)

            def tile_low(j):
                dve.wait_ge(thi_done, j.n + 1)
                nc.vector.tensor_tensor(out=xt_lo[:, j.i % 2], in0=xt_ps[j.i % 2][:, 0:TR], in1=xt_hi[:, j.i % 2],
                                        op=ALU.subtract).then_inc(tlo_done, 1)

            def hidden_second(j, e):
                dve.wait_ge(z_done[1], j.n + 1)
                if type(j.n) is not int or j.n >= 2:
                    dve.wait_ge(y_done, j.n - 1)
                nc.vector.tensor_scalar(out=hid[1][:, j.i % 2], in0=z_ps[1][j.i % 2][:, 0:TR], scalar1=b1_sb[:, bass.ds(HC * e + 1, 1)],
                                        scalar2=0.0, op0=ALU.add, op1=ALU.max).then_inc(h_ready[1], 1)

            def keep_y(j, e):
                dve.wait_ge(y_done, j.n + 1)
                if type(j.n) is not int or j.n >= NX:
                    dve.wait_ge(y_stored[j.i], 16 * j.g)
                nc.vector.tensor_tensor(out=y_tile[:, j.i], in0=y_ps[j.i % 2][:, 0:TR].rearrange("p (t d) -> p t d", d=D),
                                        in1=b2_sb[:, bass.ds(e, 1)].to_broadcast([P, TT, D]), op=ALU.add).then_inc(y_kept, 1)

            def tile_body(j, own, ahead):
                if later(j, 2):
                    tile_low(later(j, 2))
                if later(j, 1):
                    hidden_second(later(j, 1), ahead)
                keep_y(j, own)
                if type(j.n) is int and j.n < NX:
                    y_slots_part(j.n)

            tile_low(tile(0))
            tile_low(tile(1))
            hidden_second(tile(0), experts_of(VECTOR, 0, 1)[0])
            over_tiles(dve, tile_body, 2, experts_two(VECTOR))

            over_blocks(dve, qbody, 2)
            end = Block(NBLK - 1, PER - 1, NB - 1)
            query_low(end, NP - 1)
            denominators(end)
            reciprocals(end)
            divide(end)
            residual(end)

        @block.tensor
        def _(pe):
            nc.tensor.sem_inc(e_free, NE)
            pe.wait_ge(w_sp, 16 * len(early_sp))
            mm = nc.tensor.matmul

            def turn_x(b):
                pe.wait_ge(xn_ready, b.n + 1)
                if not (type(b.n) is int and b.n == 0):
                    pe.wait_ge(kst_ready, NH * b.n)
                for t in range(BT):
                    last = nc.tensor.transpose(xk[:, t * P:(t + 1) * P], xn[:, b.k, t], ident_sb[:])
                last.then_inc(xT_done, 1)

            def keys(b, a):
                if a == 0:
                    pe.wait_ge(xT_kept, b.n + 1)
                else:
                    pe.wait_ge(kst_ready, NH * b.n + a)
                mm(xk[:, :], wk_sb[:, a], xnT[:, b.k], start=True, stop=True).then_inc(kT_done, 1)

            def values(b, j):
                if j:
                    pe.wait_ge(v_taken, 2 * b.n + j)
                elif not (type(b.n) is int and b.n == 0):
                    pe.wait_ge(rank_ready, b.n)
                w = D + E
                for t in range(2):
                    last = mm(vb[:, t * w:(t + 1) * w], xnT[:, b.k, (2 * j + t) * P:(2 * j + t + 1) * P], wvg_sb[:],
                              start=(t == 0), stop=(t == 1), skip_group_check=True)
                last.then_inc(v_done, 1)

            def key_features(b, u):
                a, t = divmod(u, BT)
                if t == 0:
                    pe.wait_ge(kst_ready, NH * b.n + a + 1)
                pe.wait_ge(dp_free, UN * b.n + u + 1)
                w = stack[:, b.k, a, t * P:(t + 1) * P]
                mm(dp[u % 4][:, :], w, feat_hi[:], start=True, stop=False, skip_group_check=True)
                mm(dp[u % 4][:, :], w, feat_lo[:], start=False, stop=False, skip_group_check=True).then_inc(feat_done, 1)

            def turn_max(b, u):
                pe.wait_ge(mx_ready, UN * b.n + u + 1)
                pe.wait_ge(mxT_ready, ONE + UN * b.n + u)
                nc.tensor.transpose(mt16, mx16[:, u % NM], ident16[:]).then_inc(mxT_done, 1)

            def shift(b, u):
                pe.wait_ge(mxT_ready, ONE + UN * b.n + u + 1)
                mm(dp[u % 4][:, :], mxT[:, u % 2], sel_sb[:], start=False, stop=True, skip_group_check=True).then_inc(shifted, 1)

            def kv(b, u):
                a, t = divmod(u, BT)
                on_pool, count = low_count(KEYS_POOL, b.n, u)
                pe.wait_ge(elo_ready[on_pool], count)
                if a == 0:
                    pe.wait_ge(vlo_done, 2 * b.n + t // 2 + 1)
                if b.k == 0 and u == 0:
                    pe.wait_ge(kv_taken, ONE + b.batch)
                for n in range(PH):
                    pr = a * PH + n
                    mm(kv_ps[:, pr].rearrange("p s c -> p (s c)"), e_hi[:, u % NE, n * P:(n + 1) * P],
                       v16[:, b.k, t, pr].rearrange("p s c -> p (s c)"), start=(b.k == 0 and u == 0 and n == 0),
                       stop=False, skip_group_check=True)
                    if on_pool:
                        mm(kv_ps[:, pr].rearrange("p s c -> p (s c)"), eps_hi[:], v16[:, b.k, t, pr].rearrange("p s c -> p (s c)"),
                           start=False, stop=False, skip_group_check=True)
                        mm(kv_ps[:, pr, 0], eps_lo[:], v16[:, b.k, t, pr, 0], start=False, stop=False, skip_group_check=True)
                    last = mm(kv_ps[:, pr, 0], e_lo[:, u % NE, n * P:(n + 1) * P], v16[:, b.k, t, pr, 0],
                              start=False, stop=(b.k == PER - 1 and u == UN - 1 and n == PH - 1), skip_group_check=True)
                last.then_inc(e_free, 1)

            def rank_in_block(b):
                pe.wait_ge(chosen_ready, b.n + 1)
                if not (type(b.n) is int and b.n == 0):
                    pe.wait_ge(rank_ready, b.n)
                c = chosen[:].rearrange("p t e -> p (t e)")
                mm(rank_ps, below_sb[:], c, start=True, stop=False, skip_group_check=True)
                for t in range(1, BT + 1):
                    last = mm(rank_ps[:, t * E:], ones_sb[:], c[:, 0:(BT + 1 - t) * E], start=False, stop=(t == BT), skip_group_check=True)
                last.then_inc(rank_done, 1)

            def body(b):
                nb = after(b)
                for s in range(UN):
                    if at := step_of(b, s, TURN_LAG, UN):
                        turn_max(*at)
                    key_features(b, s)
                    if at := step_of(b, s, TURN_LAG, UN):
                        shift(*at)
                    if at := step_of(b, s, KV_LAG, UN):
                        kv(*at)
                    if s == RANK_STEP:
                        rank_in_block(b)
                    if s == 0 and step_of(b, 0, UN, UN):
                        keys(b, 1)
                    if nb and s == XT_STEP:
                        turn_x(nb)
                    if nb and s == KT_STEP:
                        values(nb, 0)
                        keys(nb, 0)
                    if nb and s == KT_STEP + 1:
                        values(nb, 1)

            z = Block(0, 0, 0)
            turn_x(z)
            pe.wait_ge(s_const, 2)
            pe.wait_ge(w_act, 16 * len(early_act))
            keys(z, 0)
            values(z, 0)
            keys(z, 1)
            values(z, 1)
            over_blocks(pe, body, 1)
            end = Block(NBLK - 1, PER - 1, NB - 1)
            for u in range(UN - TURN_LAG, UN):
                turn_max(end, u)
                shift(end, u)
            for u in range(UN - KV_LAG, UN):
                kv(end, u)

            pe.wait_ge(w_late, 16 * len(late))
            nc.tensor.sem_inc(qe_free, NE)
            pe.wait_ge(dp_free, 4 + UN * NBLK)
            pe.wait_ge(kv_split, ONE + 2 * NB)

            def queries(b, a):
                if a == 1:
                    pe.wait_ge(qst_ready, NH * b.n + 1)
                elif not (type(b.n) is int and b.n == 0):
                    pe.wait_ge(qst_ready, NH * b.n)
                mm(qb[:, :], wq_sb[:, a], xnT_all[:, bass.ds(b.n, 1)].rearrange("p o n -> p (o n)"),
                   start=True, stop=True).then_inc(qT_done, 1)

            def qfeat(b, u):
                a, t = divmod(u, BT)
                if t == 0:
                    pe.wait_ge(qst_ready, NH * b.n + a + 1)
                if not (type(b.n) is int and b.n == 0 and u < 2):
                    pe.wait_ge(qmx_step, UN * b.n + u - 1)
                w = stack[:, b.k, a, t * P:(t + 1) * P]
                mm(tm[u % 2][:, :], w, feat_hi[:], start=True, stop=False)
                mm(tm[u % 2][:, :], w, feat_lo[:], start=False, stop=True).then_inc(qf_done, 1)

            def qturn(b, u):
                pe.wait_ge(qmx_ready, UN * b.n + u + 1)
                if u or not (type(b.n) is int and b.n == 0):
                    pe.wait_ge(qmxT_ready, UN * b.n + u)
                nc.tensor.transpose(mt16, mx16[:, u % NM], ident16[:]).then_inc(qmxT_done, 1)

            def qshifted(b, j):
                a, n = divmod(j, PH)
                if n == 0:
                    pe.wait_ge(qmxT_ready, UN * b.n + (a + 1) * BT)
                pe.wait_ge(qs_free, NP * b.n + j + 1)
                f = slice(n * P, (n + 1) * P)
                mm(fm[j % 2][:, :], feat_hi[:, f], stack[:, b.k, a], start=True, stop=False)
                mm(fm[j % 2][:, :], feat_lo[:, f], stack[:, b.k, a], start=False, stop=False)
                mm(fm[j % 2][:, :], sel_sb[:, f], mxT_q[:, b.k, a], start=False, stop=True).then_inc(qs_done, 1)

            def weigh(b, j):
                on_pool, count = low_count(QUERIES_POOL, b.n, j)
                pe.wait_ge(qlo_ready[on_pool], count)
                if j == 0:
                    pe.wait_ge(res_ready, ONE + b.n)
                    if b.k == 0:
                        pe.wait_ge(kv_now_ready, b.batch + 1)
                for t in range(BT):
                    o = ob[t // 2][:, (t % 2) * H * C + j * 2 * C:(t % 2) * H * C + (j + 1) * 2 * C]
                    c = slice(t * P, (t + 1) * P)
                    mm(o, e_hi[:, j % NE, c], kv_now[:, j, 0], start=(j == 0 and t % 2 == 0), stop=False, skip_group_check=True)
                    mm(o, e_hi[:, j % NE, c], kv_now[:, j, 1], start=False, stop=False, skip_group_check=True)
                    if on_pool:
                        mm(o, eps_hi[:], kv_now[:, j, 0], start=False, stop=False, skip_group_check=True)
                        mm(o, eps_hi[:], kv_now[:, j, 1], start=False, stop=False, skip_group_check=True)
                        mm(o, eps_lo[:], kv_now[:, j, 0], start=False, stop=False, skip_group_check=True)
                    last = mm(o, e_lo[:, j % NE, c], kv_now[:, j, 0], start=False, stop=(j == NP - 1 and t % 2 == 1), skip_group_check=True)
                last.then_inc(qe_free, 1)

            def turn_attn(b):
                pe.wait_ge(attn_ready, ONE + b.n + 1)
                for t in range(BT):
                    last = nc.tensor.transpose(ob[0][:, t * P:(t + 1) * P], attn[:, t], ident_sb[:])
                last.then_inc(aT_done, 1)

            def project(b):
                pe.wait_ge(aT_ready, b.n + 1)
                for t in range(BT):
                    last = mm(ob[1][:, t * P:(t + 1) * P], attnT[:, t * P:(t + 1) * P], wp_sb[:], start=(t == 0), stop=(t == BT - 1),
                              skip_group_check=True)
                last.then_inc(proj_done, 1)

            def qbody(b):
                nb, nnb = after(b), after(b, 2)
                before = step_of(b, 0, UN, UN)
                before = before[0] if before else None
                for s in range(NP):
                    qshifted(b, s)
                    if before and s == AT_STEP:
                        turn_attn(before)
                    if at := turned(b, s):
                        qturn(*at)
                    if nb:
                        qfeat(nb, s)
                    if s >= WEIGH_STEP:
                        weigh(b, 2 * (s - WEIGH_STEP))
                        weigh(b, 2 * (s - WEIGH_STEP) + 1)
                    elif before and s < NP // 2 - (NP - WEIGH_STEP):
                        weigh(before, 2 * (s + NP - WEIGH_STEP))
                        weigh(before, 2 * (s + NP - WEIGH_STEP) + 1)
                    if before and s == PROJ_STEP:
                        project(before)
                    if nb and s == Q1_STEP:
                        queries(nb, 1)
                    if nnb and s == Q0_STEP:
                        queries(nnb, 0)

            z = Block(0, 0, 0)
            queries(z, 0)
            queries(z, 1)
            qfeat(z, 0)
            qfeat(z, 1)
            for u in range(UN):
                qturn(z, u)
                if u + 2 < UN:
                    qfeat(z, u + 2)
            queries(after(z), 0)

            pe.wait_ge(w_ready, 2)
            pe.wait_ge(qst_ready, NH + 1)

            def turn_tile(j):
                pe.wait_ge(tile_in[j.i], 16 * j.g + 16)
                if type(j.n) is not int or j.n >= 2:
                    pe.wait_ge(tlo_done, j.n - 1)
                for t in range(TT):
                    last = nc.tensor.transpose(xt_ps[j.i % 2][:, t * P:(t + 1) * P], x_tile[:, j.i, t], ident_sb[:])
                last.then_inc(tile_turned, 1)

            def hidden(j, e):
                pe.wait_ge(tlo_done, j.n + 1)
                hi, lo = xt_hi[:, j.i % 2], xt_lo[:, j.i % 2]
                for c in range(HC):
                    o, w = z_ps[c][j.i % 2][:, 0:TR], [v[:, bass.ds(e, 1), c * P:(c + 1) * P] for v in (w1_hi, w1_lo)]
                    mm(o, w[0], hi, start=True, stop=False)
                    mm(o, w[0], lo, start=False, stop=False)
                    mm(o, w[1], hi, start=False, stop=True).then_inc(z_done[c], 1)

            def result(j, e):
                pe.wait_ge(h_ready[0], j.n + 1)
                pe.wait_ge(h_ready[1], j.n + 1)
                if type(j.n) is not int or j.n >= 2:
                    pe.wait_ge(y_kept, j.n - 1)
                for t in range(TT):
                    for c in range(HC):
                        last = mm(y_ps[j.i % 2][:, t * P:(t + 1) * P], hid[c][:, j.i % 2, t * P:(t + 1) * P],
                                  w2_sb[:, bass.ds(HC * e + c, 1)], start=(t == 0 and c == 0), stop=(t == TT - 1 and c == HC - 1),
                                  skip_group_check=True)
                last.then_inc(y_done, 1)

            def tile_body(j, own, ahead):
                if later(j, 2):
                    turn_tile(later(j, 2))
                if later(j, 1):
                    hidden(later(j, 1), ahead)
                result(j, own)

            turn_tile(tile(0))
            turn_tile(tile(1))
            hidden(tile(0), experts_of(TENSOR, 0, 1)[0])
            over_tiles(pe, tile_body, 2, experts_two(TENSOR))
            pe.wait_ge(y_kept, TILES)

            over_blocks(pe, qbody, 2)
            end = Block(NBLK - 1, PER - 1, NB - 1)
            for j in range(2 * (NP - WEIGH_STEP), NP):
                weigh(end, j)
            turn_attn(end)
            project(end)


_SHAPES = dict(D=128, H=16, M=64, E=8, HF=256, K=2, TR=256)


def kernel(L0_attn_x, L0_attn_qkv_w, L0_attn_qkv_b, L0_attn_proj_w, L0_attn_proj_b, L0_attn_projection_matrix,
           L0_ffn_Wg, L0_ffn_W1, L0_ffn_b1, L0_ffn_W2, L0_ffn_b2):
    import numpy as np
    import concourse.bacc as bacc
    from concourse.bass_utils import run_bass_kernel_spmd
    D, H, M, E, HF, K, TR = (_SHAPES[k] for k in ("D", "H", "M", "E", "HF", "K", "TR"))
    HD, HH = D // H, H // 2
    a = [np.asarray(v) for v in (L0_attn_x, L0_attn_qkv_w, L0_attn_qkv_b, L0_attn_proj_w, L0_attn_proj_b,
                                 L0_attn_projection_matrix, L0_ffn_Wg, L0_ffn_W1, L0_ffn_b1, L0_ffn_W2, L0_ffn_b2)]
    x, qkv_w, qkv_b, proj_w, proj_b, pm, wg, w1, b1, w2, b2 = a

    def twice(w):
        h = w.reshape(2, D // 2, -1)
        return np.concatenate([h, h], axis=1)

    feat = np.zeros((2, HH, HD, HH, M), pm.dtype)
    for h in range(HH):
        feat[:, h, :, h, :] = pm.T
    sel = np.zeros((128, HH, M), np.float16)
    for h in range(HH):
        sel[[h, HH + h], h, :] = 1
    low = np.zeros((128, 1), np.float32)
    low[64:] = 1
    tiles = x.shape[0] * x.shape[1] * K // TR + E - 1
    arrays = {
        "x": x,
        "wk2": twice(qkv_w[D:2 * D]).transpose(2, 0, 1),
        "wq2": twice(qkv_w[0:D]).transpose(2, 0, 1),
        "wvg": np.concatenate([qkv_w[2 * D:].T, wg], axis=1),
        "bk2": twice(qkv_b[D:2 * D])[:, :, 0].T,
        "bq2": twice(qkv_b[0:D])[:, :, 0].T,
        "bv": np.broadcast_to(qkv_b[2 * D:], (128, D)),
        "wp": proj_w.T,
        "bp": np.broadcast_to(proj_b, (128, D)),
        "feat": feat.reshape(128, HH * M),
        "sel": sel.reshape(128, HH * M),
        "split": low,
        "ident": np.eye(128, dtype=np.float32),
        "w1": w1.transpose(1, 0, 2),
        "b1": b1.reshape(E * HF // 128, 128).T,
        "w2": w2.reshape(E * HF // 128, 128, D).transpose(1, 0, 2),
        "b2": np.broadcast_to(b2, (128, E, D)),
        "lanes": np.broadcast_to(np.arange(E, 0, -1, dtype=np.float32), (128, E)),
        "tile_no": np.broadcast_to(np.arange(tiles, dtype=np.float32), (128, tiles)),
        "below": np.triu(np.ones((128, 128), np.float16), 1),
        "ones": np.ones((128, 128), np.float16),
    }
    nc = bacc.Bacc("TRN2", target_bir_lowering=False, num_devices=1)
    ins, aps = {}, []
    for name, v in arrays.items():
        v = np.ascontiguousarray(v)
        ins[f"in_{name}"] = v
        aps.append(nc.dram_tensor(f"in_{name}", v.shape, mybir.dt.from_np(v.dtype), kind="ExternalInput").ap())
    out = nc.dram_tensor("out_0", x.shape, mybir.dt.from_np(x.dtype), kind="ExternalOutput").ap()
    favor_moe_block(nc, *aps, out)
    r = run_bass_kernel_spmd(nc, [ins], core_ids=[0])
    return r.results[0]["out_0"]
```
